# Optimizing a Trainium2 kernel written in Bass

```python
import numpy as np
import jax
import jax.numpy as jnp

def _softmax(x, axis=-1):
    return jax.nn.softmax(x, axis=axis)

def _gelu(x):
    return jax.nn.gelu(x, approximate=True)

def _silu(x):
    return jax.nn.silu(x)

def _sigmoid(x):
    return jax.nn.sigmoid(x)

def _layernorm(x, axis=-1, eps=1e-05):
    m = jnp.mean(x, axis=axis, keepdims=True)
    v = jnp.var(x, axis=axis, keepdims=True)
    return (x - m) / jnp.sqrt(v + eps)

def _scatter_add(tgt, idx, src, axis=0):
    return tgt.at[idx].add(src)

def _segment_sum(src, seg, n):
    return jax.ops.segment_sum(src, seg, n)
kernel_name = 'mk_gnn_resnorm_d2_gnn_r8_69204c'

def setup_inputs(seed: int=0):
    np.random.seed(seed)
    _w = jnp.asarray

    def _rec_inputs():
        import jax
        import jax.numpy as jnp
        _gk = jax.random.key(seed)
        x = -0.0001006 + 1 * jax.random.normal(jax.random.fold_in(_gk, 1), (6250, 96), jnp.float32)
        src = jax.random.randint(jax.random.fold_in(_gk, 2), (200000,), 0, 6250, jnp.int32)
        dst = jnp.minimum((6250 * jax.random.uniform(jax.random.fold_in(_gk, 3), (200000,)) ** 2.0).astype(jnp.int32), 49999)
        _o = jnp.argsort(dst, stable=True)
        src = src[_o]
        dst = dst[_o]
        edge_attr_96 = -4.21973e-06 + 0.0999841 * jax.random.normal(jax.random.fold_in(_gk, 12), (200000, 96), jnp.float32)
        return (x, src, dst, edge_attr_96)
    x, src, dst, edge_attr_96 = _rec_inputs()

    def _L0_gnn_setup():
        import jax, jax.numpy as jnp
        import numpy as np
        N_NODES = 6250
        N_EDGES = 100000
        D_IN = 96
        D_OUT = 96
        NEG_SLOPE = 0.2
        key = jax.random.key(seed)
        k1, k2, k3, k4, k5 = jax.random.split(key, 5)
        x = jax.random.normal(k1, (N_NODES, D_IN), dtype=jnp.float32)
        W = jax.random.normal(k2, (D_IN, D_OUT), dtype=jnp.float32) * (1.0 / np.sqrt(D_IN))
        att_src = jax.random.normal(k3, (D_OUT,), dtype=jnp.float32) * 0.1
        att_dst = jax.random.normal(k4, (D_OUT,), dtype=jnp.float32) * 0.1
        bias = jnp.zeros((D_OUT,), dtype=jnp.float32)
        edge_index = jax.random.randint(k5, (2, N_EDGES), 0, N_NODES, dtype=jnp.int64)
        return {'x': x, 'W': W, 'att_src': att_src, 'att_dst': att_dst, 'bias': bias, 'edge_index': edge_index}
    _L0_gnn_all = _L0_gnn_setup()
    _L0_gnn_in = {k: v for k, v in _L0_gnn_all.items() if k in ('W', 'att_src', 'att_dst', 'bias')}
    del _L0_gnn_all

    def _L1_gnn_setup():
        import jax, jax.numpy as jnp
        import numpy as np
        N_NODES = 6250
        N_EDGES = 100000
        HID = 96

        def _gelu(x):
            return jax.nn.gelu(x, approximate=False)
        key = jax.random.key(seed)
        ks = jax.random.split(key, 12)
        s = 1.0 / np.sqrt(HID)
        return {'x_feat': jax.random.normal(ks[0], (N_NODES, HID), jnp.float32), 'bases': jax.random.normal(ks[1], (N_EDGES, HID), jnp.float32) * 0.1, 'W_pre': jax.random.normal(ks[2], (HID, HID), jnp.float32) * s, 'b_pre': jax.random.normal(ks[3], (HID,), jnp.float32) * s, 'W1': jax.random.normal(ks[4], (HID, HID), jnp.float32) * s, 'b1': jax.random.normal(ks[5], (HID,), jnp.float32) * s, 'W2': jax.random.normal(ks[6], (HID, HID), jnp.float32) * s, 'b2': jax.random.normal(ks[7], (HID,), jnp.float32) * s, 'src': jax.random.randint(ks[8], (N_EDGES,), 0, N_NODES, jnp.int32), 'dst': jax.random.randint(ks[9], (N_EDGES,), 0, N_NODES, jnp.int32)}
    _L1_gnn_all = _L1_gnn_setup()
    _L1_gnn_in = {k: v for k, v in _L1_gnn_all.items() if k in ('W_pre', 'b_pre', 'W1', 'b1', 'W2', 'b2')}
    del _L1_gnn_all
    return {'x': x, 'src': src, 'dst': dst, 'edge_attr_96': edge_attr_96, 'L0_gnn_W': _L0_gnn_in['W'], 'L0_gnn_att_src': _L0_gnn_in['att_src'], 'L0_gnn_att_dst': _L0_gnn_in['att_dst'], 'L0_gnn_bias': _L0_gnn_in['bias'], 'L1_gnn_W_pre': _L1_gnn_in['W_pre'], 'L1_gnn_b_pre': _L1_gnn_in['b_pre'], 'L1_gnn_W1': _L1_gnn_in['W1'], 'L1_gnn_b1': _L1_gnn_in['b1'], 'L1_gnn_W2': _L1_gnn_in['W2'], 'L1_gnn_b2': _L1_gnn_in['b2']}

def reference(x, src, dst, edge_attr_96, L0_gnn_W, L0_gnn_att_src, L0_gnn_att_dst, L0_gnn_bias, L1_gnn_W_pre, L1_gnn_b_pre, L1_gnn_W1, L1_gnn_b1, L1_gnn_W2, L1_gnn_b2):
    import jax
    import jax.numpy as jnp

    def _L0_gnn_ref(x, W, att_src, att_dst, bias, edge_index):
        import jax, jax.numpy as jnp
        import numpy as np
        N_NODES = 6250
        N_EDGES = 100000
        D_IN = 96
        D_OUT = 96
        NEG_SLOPE = 0.2
        N = x.shape[0]
        h = x @ W
        loops = jnp.arange(N, dtype=edge_index.dtype)
        src = jnp.concatenate([edge_index[0], loops])
        dst = jnp.concatenate([edge_index[1], loops])
        a_src = h @ att_src
        a_dst = h @ att_dst
        e = jax.nn.leaky_relu(a_src[src] + a_dst[dst], NEG_SLOPE)
        m = jax.ops.segment_max(e, dst, num_segments=N)
        e = jnp.exp(e - m[dst])
        denom = jax.ops.segment_sum(e, dst, num_segments=N)
        alpha = e / (denom[dst] + 1e-16)
        out = jax.ops.segment_sum(h[src] * alpha[:, None], dst, num_segments=N)
        return jnp.tanh(out + bias)

    def _L1_gnn_ref(x_feat, bases, W_pre, b_pre, W1, b1, W2, b2, src, dst):
        import jax, jax.numpy as jnp
        import numpy as np
        N_NODES = 6250
        N_EDGES = 100000
        HID = 96

        def _gelu(x):
            return jax.nn.gelu(x, approximate=False)
        n = x_feat.shape[0]
        h = _gelu(x_feat @ W_pre + b_pre)
        msg = h[src] * bases
        aggr = jax.ops.segment_sum(msg, dst, num_segments=n)
        x = x_feat + aggr
        y = _gelu(_gelu(x @ W1 + b1) @ W2 + b2)
        return x + y
    edge_index = jnp.stack([src, dst])
    x = _layernorm(x + _L0_gnn_ref(x, L0_gnn_W, L0_gnn_att_src, L0_gnn_att_dst, L0_gnn_bias, edge_index), axis=-1)
    x = _layernorm(x + _L1_gnn_ref(x, edge_attr_96, L1_gnn_W_pre, L1_gnn_b_pre, L1_gnn_W1, L1_gnn_b1, L1_gnn_W2, L1_gnn_b2, src, dst), axis=-1)
    return x

_drawn_inputs = setup_inputs


def setup_inputs(seed=0):
    import zlib

    import numpy as np

    out = dict(_drawn_inputs(seed))
    spreads = {'L0_gnn_bias': (0.0, 0.1)}
    factors = {'L1_gnn_b_pre': 3.024}
    for name, (base, spread) in spreads.items():
        noise = np.random.default_rng([zlib.crc32(name.encode()), seed]).standard_normal(out[name].shape)
        drawn = base * np.exp(spread * noise) if base else spread * noise
        out[name] = jnp.asarray(drawn.astype(out[name].dtype))
    for name, factor in factors.items():
        out[name] = (out[name] * factor).astype(out[name].dtype)
    return out
```

```python
from contextlib import ExitStack

import concourse.bass as bass
from concourse import mybir

FP32 = mybir.dt.float32
INT32 = mybir.dt.int32
ALU = mybir.AluOpType
ACT = mybir.ActivationFunctionType
AX = mybir.AxisListType

P = 128
TILES = 8
SLOTS = 3
WIN = 72
NEG = -1e30
SLOPE = 0.2
EPS = 1e-5
CB = 4


def gnn(nc, x, src, dst, edge_attr, w0, att_src, att_dst, bias0, w_pre, b_pre, w1, b1, w2, b2, out):
    N, D = x.shape
    E = src.shape[0]
    GE = P * TILES
    GROUPS = -(-E // GE)
    ROUNDS = (GROUPS - 1) // SLOTS
    LAST = GROUPS - 1
    LAST_P = (E - LAST * GE) // TILES
    assert LAST == ROUNDS * SLOTS and LAST_P * TILES == E - LAST * GE
    D1 = D + 1
    D2 = D + 2
    CN = CB * P
    CHUNKS = -(-N // CN)
    LAST_N = N - (CHUNKS - 1) * CN
    assert LAST_N <= P and CHUNKS % 2 == 1
    NP = CHUNKS * CN
    assert NP >= N + WIN
    TG = GROUPS // 2
    assert GROUPS == 2 * TG and TG <= P
    MAXW = -(-(N - 1) // WIN)

    ctx = ExitStack()
    with ctx:
        def sb(name, shape, dt=FP32):
            return ctx.enter_context(nc.sbuf_tensor(name, shape, dt))

        def sem(name):
            return ctx.enter_context(nc.semaphore(name))

        def sems(name, n):
            return [sem(f"{name}{i}") for i in range(n)]

        table0 = nc.dram_tensor("table0", (N, D2), FP32, kind="Internal").ap()
        table1 = nc.dram_tensor("table1", (N, D), FP32, kind="Internal").ap()

        iota = sb("iota", [P, NP], INT32)
        adst = sb("adst", [P, NP])
        peak = sb("peak", [P, NP])
        acc = sb("acc", [D1, NP])
        x1 = sb("x1", [P, NP // P, D])

        src_i = sb("src_i", [P, SLOTS, TILES], INT32)
        dst_i = sb("dst_i", [P, SLOTS, TILES], INT32)
        rows = sb("rows", [P, SLOTS, TILES * D2])
        attr = sb("attr", [P, SLOTS, TILES * D])
        onehot = sb("onehot", [P, SLOTS, TILES * WIN])

        other = sb("other", [P, TILES * WIN])
        score = sb("score", [P, TILES * WIN])
        weight = sb("weight", [P, TILES * WIN])
        top = sb("top", [P, WIN])
        top_col = sb("top_col", [WIN, 1])
        top_diag = sb("top_diag", [WIN, WIN])
        cand = sb("cand", [P, WIN])
        newp = sb("newp", [P, WIN])
        drop = sb("drop", [D1, WIN])
        fade = sb("fade", [D1, WIN])
        fade_x = sb("fade_x", [D1, WIN])
        onehot_x = sb("onehot_x", [P, TILES * WIN])

        ident = sb("ident", [P, P])
        ones = sb("ones", [P, P])
        zeros = sb("zeros", [P, P])
        w0x = sb("w0x", [D1, D2])
        w0t = sb("w0t", [D, D])
        att = sb("att", [D, 2])
        w0att = sb("w0att", [D, 2])
        w0dst = sb("w0dst", [D, P])
        w0both = sb("w0both", [D, P])
        bias_b = sb("bias_b", [P, D])
        w_prex = sb("w_prex", [D1, D])
        w1s = sb("w1s", [D, D])
        w2s = sb("w2s", [D, D])
        b1s = sb("b1s", [D, 1])
        b2s = sb("b2s", [D, 1])

        xs = sb("xs", [P, 2, CB * D])
        colw = sb("colw", [D1, 2, CN])
        colv = sb("colv", [D1, 2, CN])
        zcol = sb("zcol", [P, 2, CN])
        rowt = sb("rowt", [P, 2, CB * D2])
        rowu = sb("rowu", [P, 2, CB * D])
        sq = sb("sq", [P, CB * D])
        stat = sb("stat", [P, 4, CB])
        minus_half = sb("minus_half", [P, CB])
        stat_d = sb("stat_d", [P, 2, CB])

        dsts = sb("dsts", [TG, 2, GE], INT32)
        low = sb("low", [TG, 2])
        high = sb("high", [TG, 2])
        steps_i = sb("steps_i", [TG, MAXW], INT32)
        more = sb("more", [TG, 2, MAXW])
        extra = sb("extra", [TG, 2])
        line = sb("line", [1, 2, GROUPS])
        upto = sb("upto", [1, GROUPS])
        run = sb("run", [1, GROUPS])
        win_tab = sb("win_tab", [1, 3, GROUPS], INT32)

        bank = [ctx.enter_context(nc.psum_tensor(f"bank{i}", [P, 512], FP32)) for i in range(8)]

        s_x = sem("s_x")
        s_w = sem("s_w")
        s_dsts = sem("s_dsts")
        s_const = sem("s_const")
        s_fill = sem("s_fill")
        s_prep = sem("s_prep")
        s_prepc = sem("s_prepc")
        s_line = sem("s_line")
        s_tab0 = sem("s_tab0")
        s_tab = sem("s_tab")
        s_v = sem("s_v")

        a_x = sem("a_x")
        a_t = sem("a_t")
        a_tc = sem("a_tc")
        a_row = sem("a_row")
        a_rowc = sem("a_rowc")
        a_col = sem("a_col")
        a_colc = sem("a_colc")
        a_peak = sem("a_peak")
        a_st = sems("a_st", 2)
        a_free = sem("a_free")
        m_col = sem("m_col")
        m_t = sem("m_t")
        m_u = sem("m_u")
        m_th = sem("m_th")
        m_x1 = sem("m_x1")
        m_x1c = sem("m_x1c")
        m_x1t = sem("m_x1t")
        m_colw = sem("m_colw")
        m_h = sem("m_h")
        m_g = sem("m_g")
        m_st = sems("m_st", 2)
        m_free = sem("m_free")
        m_var = sem("m_var")
        m_rstd = sem("m_rstd")
        m_v = sem("m_v")
        m_va = sem("m_va")
        f_y1 = sem("f_y1")
        f_g1 = sem("f_g1")
        f_y2 = sem("f_y2")
        f_g2 = sem("f_g2")
        f_s = sem("f_s")
        f_t = sem("f_t")
        f_o = sem("f_o")
        f_st = sems("f_st", 2)
        f_free = sem("f_free")
        f_var = sem("f_var")
        f_rstd = sem("f_rstd")
        f_v = sem("f_v")

        class Edge:
            def __init__(self, n):
                self.src = sems(f"e{n}_src", SLOTS)
                self.dst = sems(f"e{n}_dst", SLOTS)
                self.attr = sems(f"e{n}_attr", SLOTS)
                self.rows = sems(f"e{n}_rows", SLOTS)
                self.go = sem(f"e{n}_go")
                self.free = sem(f"e{n}_free")
                self.pad = sem(f"e{n}_pad")
                self.acc = sem(f"e{n}_acc")
                self.v = sem(f"e{n}_v")

        class Top:
            def __init__(self, n):
                self.top = sem(f"{n}_top")
                self.topt = sem(f"{n}_topt")
                self.diag = sem(f"{n}_diag")
                self.topb = sem(f"{n}_topb")
                self.score = sem(f"{n}_score")
                self.w = sem(f"{n}_w")

        e0, e1 = Edge(0), Edge(1)
        t0, tx = Top("t0"), Top("tx")
        x0_acc, x1_acc = sem("x0_acc"), sem("x1_acc")
        x0_v, x1_v = sem("x0_v"), sem("x1_v")
        e1_hot, e1_msg, x1_hot = sem("e1_hot"), sem("e1_msg"), sem("x1_hot")

        p_top, px_top = bank[0][0:WIN, 0:P], bank[3][0:WIN, 0:P]
        p_topb, px_topb = bank[1][:, 0:WIN], bank[4][:, 0:WIN]
        p_acc0, px_acc0 = bank[2][0:D1, 0:WIN], bank[5][0:D1, 0:WIN]
        p_acc1, px_acc1 = [bank[i][0:D, 0:WIN] for i in range(SLOTS)], bank[5][0:D, 0:WIN]

        def by_tile(t):
            return t.rearrange("p (j n) -> p j n", j=TILES)

        def rows0(u):
            return rows[:, u, :].rearrange("p (j d) -> p j d", j=TILES)

        def rows1(u):
            return rows[:, u, 0:TILES * D].rearrange("p (j d) -> p j d", j=TILES)

        def over_tiles(t):
            return t[:, None, :].broadcast_to([P, TILES, WIN])

        def over_window(t):
            return t[:, :, None].broadcast_to([P, TILES, WIN])

        def by_block(t, w=D):
            return t[:, 0:CB * w].rearrange("p (b d) -> p b d", d=w)

        def over_rows(t):
            return t[:, :, None].broadcast_to([P, CB, D])

        def columns(c):
            return bass.ds(c * CN, CN)

        def groups(eng, body):
            with eng.Fori(0, ROUNDS) as it:
                for u in range(SLOTS):
                    body(it * SLOTS + u, it, u)
            return body(LAST, ROUNDS, 0)

        def chunks(eng, ahead, rest):
            if ahead:
                ahead(0, 0)
            with eng.Fori(0, CHUNKS // 2) as it:
                for u in range(2):
                    if ahead:
                        ahead(it * 2 + u + 1, 1 - u)
                    rest(it * 2 + u, u)
            rest(CHUNKS - 1, 0)

        class Steps:
            def __init__(self, eng, s, base, most):
                self.eng, self.s, self.base, self.n, self.most = eng, s, base, 0, most

            def step(self, ins):
                self.n += 1
                assert self.n <= self.most
                ins.then_inc(self.s, 1)

            def wait(self, n=None):
                self.eng.wait_ge(self.s, self.base + (n or self.n))

            def link(self, ins):
                self.step(ins)
                self.wait()

            def done(self):
                assert self.n == self.most

        block = ctx.enter_context(nc.Block())

        @block.sync
        def _(sp):
            FULL = N // P
            sp.dma_start(w0x[0:D, 0:D], w0).then_inc(s_w, 16)
            sp.wait_ge(s_fill, 1)
            sp.dma_start(x1[:, 0:FULL, :], x[0:FULL * P, :].rearrange("(b p) d -> p b d", p=P)).then_inc(s_x, 16)
            sp.dma_start(x1[0:N - FULL * P, FULL, :], x[FULL * P:N, :]).then_inc(s_x, 16)
            sp.dma_start(att[:, 0:1], att_src.rearrange("(d a) -> d a", a=1)).then_inc(s_w, 16)
            sp.dma_start(att[:, 1:2], att_dst.rearrange("(d a) -> d a", a=1)).then_inc(s_w, 16)
            sp.dma_start(bias_b[:, :], bias0.rearrange("(a d) -> a d", a=1).broadcast_to([P, D])).then_inc(s_w, 16)
            sp.dma_start(w_prex[0:D, :], w_pre).then_inc(s_w, 16)
            sp.dma_start(w_prex[D:D1, :], b_pre.rearrange("(a d) -> a d", a=1)).then_inc(s_w, 16)
            sp.dma_start(w1s[:, :], w1).then_inc(s_w, 16)
            sp.dma_start(w2s[:, :], w2).then_inc(s_w, 16)
            sp.dma_start(b1s[:, :], b1.rearrange("(d a) -> d a", a=1)).then_inc(s_w, 16)
            sp.dma_start(b2s[:, :], b2.rearrange("(d a) -> d a", a=1)).then_inc(s_w, 16)

            def stores(dram, w, made, stored, free):
                sp.sem_inc(free, 2)
                with sp.Fori(0, CHUNKS // 2) as it:
                    for u in range(2):
                        c = it * 2 + u
                        sp.wait_ge(made, c + 1)
                        sp.dma_start(dram[bass.ds(c * CN, CN), :].rearrange("(b p) d -> p b d", p=P),
                                     by_block(rowt[:, u, :], w)).then_inc(stored[u], 16)
                        sp.wait_ge(stored[u], 16 * (it + 1))
                        sp.sem_inc(free, 1)
                sp.wait_ge(made, CHUNKS)
                sp.dma_start(dram[(CHUNKS - 1) * CN:N, :], rowt[0:LAST_N, 0, 0:w]).then_inc(stored[0], 16)
                sp.wait_ge(stored[0], 16 * (CHUNKS // 2 + 1))

            def load_edges(e, attrs):
                def body(g, it, u):
                    n = LAST_P * TILES if g is LAST else GE
                    m = n // TILES
                    sp.wait_ge(e.free, g + 1)
                    sp.dma_start(src_i[0:m, u, :], src[bass.ds(g * GE, n)].rearrange("(p j) -> p j", j=TILES))\
                        .then_inc(e.src[u], 16)
                    if g is LAST:
                        sp.wait_ge(e.pad, 1)
                    sp.dma_start(dst_i[0:m, u, :], dst[bass.ds(g * GE, n)].rearrange("(p j) -> p j", j=TILES))\
                        .then_inc(e.dst[u], 16)
                    if attrs:
                        sp.dma_start(attr[0:m, u, :],
                                     edge_attr[bass.ds(g * GE, n), :].rearrange("(p j) d -> p (j d)", j=TILES))\
                            .then_inc(e.attr[u], 16)
                return body

            stores(table0, D2, a_rowc, a_st, a_free)
            groups(sp, load_edges(e0, False))
            stores(table1, D, m_g, m_st, m_free)
            groups(sp, load_edges(e1, True))
            stores(out, D, f_o, f_st, f_free)

        @block.gpsimd
        def _(pool):
            pool.memset(ident[:, :], 0.0).then_inc(s_const, 1)
            pool.wait_ge(s_const, 1)
            pool.affine_select(out=ident[:, :], in_=ident[:, :], compare_op=ALU.not_equal, fill=1.0,
                               base=0, pattern=[[-1, P]], channel_multiplier=1).then_inc(s_const, 1)
            pool.memset(minus_half[:, :], -0.5)
            pool.iota(steps_i[:, :], pattern=[[WIN, MAXW]], base=WIN, channel_multiplier=0).then_inc(s_const, 1)
            pool.iota(iota[:, :], pattern=[[1, NP]], base=0, channel_multiplier=0).then_inc(s_const, 1)

            def gather(e, table, width):
                def body(g, it, u):
                    pool.wait_ge(e.src[u], 16 * (it + 1))
                    pool.sem_inc(e.go, 1)
                    for j in range(TILES):
                        pool.indirect_dma_start(rows[:, u, j * width:(j + 1) * width], None, table,
                                                bass.IndirectOffsetOnAxis(ap=src_i[:, u, j:j + 1], axis=0))\
                            .then_inc(e.rows[u], 16)
                return body

            def written(stored):
                pool.wait_ge(stored[0], 16 * (CHUNKS // 2 + 1))
                pool.wait_ge(stored[1], 16 * (CHUNKS // 2))

            written(a_st)
            groups(pool, gather(e0, table0, D2))

            pool.sem_inc(m_x1c, 2)

            def keep(c, u):
                pool.wait_ge(m_var, c + 1)
                pool.tensor_tensor(stat[:, 3, :], stat[:, 2, :], minus_half[:, :], ALU.pow).then_inc(m_rstd, 1)
                pool.wait_ge(m_x1, c + 1)
                pool.tensor_copy(x1[:, bass.ds(c * CB, CB), :], by_block(xs[:, u, :])).then_inc(m_x1c, 1)
            chunks(pool, None, keep)
            written(m_st)
            groups(pool, gather(e1, table1, D))

            def deviations(c, u):
                pool.wait_ge(f_var, c + 1)
                pool.tensor_tensor(stat[:, 3, :], stat[:, 2, :], minus_half[:, :], ALU.pow).then_inc(f_rstd, 1)
            chunks(pool, None, deviations)

        @block.scalar
        def _(act):
            act.dma_start(dsts[:, 0, :], dst[0:TG * GE].rearrange("(p e) -> p e", e=GE)).then_inc(s_dsts, 16)
            act.dma_start(dsts[0:TG - 1, 1, :], dst[TG * GE:LAST * GE].rearrange("(p e) -> p e", e=GE))\
                .then_inc(s_dsts, 16)
            tail = E - LAST * GE
            rep = 64
            assert (GE - tail) % rep == 0 and tail >= rep
            act.dma_start(dsts[TG - 1:TG, 1, 0:tail], dst[LAST * GE:E].rearrange("(p e) -> p e", p=1))\
                .then_inc(s_dsts, 16)
            act.dma_start(dsts[TG - 1:TG, 1, tail:GE].rearrange("p (a b) -> p a b", b=rep),
                          dst[E - rep:E].rearrange("(p a b) -> p a b", p=1, a=1)
                          .broadcast_to([1, (GE - tail) // rep, rep])).then_inc(s_dsts, 16)

            def turned(c, u):
                act.wait_ge(a_t, c + 1)
                act.activation(colw[0:D, u, :], bank[u][0:D, :], ACT.Copy).then_inc(a_tc, 1)

            def columns0(c, u):
                act.wait_ge(a_col, c + 1)
                act.activation(acc[:, columns(c)], bank[4][0:D1, :], ACT.Copy)
                act.activation(adst[:, columns(c)], bank[5][:, :], ACT.Copy)
                act.activation(zcol[:, u, :], bank[6][:, :], ACT.Copy, scale=SLOPE).then_inc(a_colc, 1)
            act.wait_ge(s_fill, 2)
            chunks(act, turned, columns0)

            def weights(g, it, u):
                act.wait_ge(t0.score, g + 1)
                act.activation(fade[:, :], drop[:, :], ACT.Exp)
                act.activation(weight[:, :], score[:, :], ACT.Exp).then_inc(t0.w, 1)
                further = act.value_load(win_tab[0:1, 1, bass.ds(g, 1)], min_val=0, max_val=MAXW)
                with act.If(further > 0):
                    before = act.value_load(win_tab[0:1, 2, bass.ds(g, 1)], min_val=0, max_val=GROUPS * MAXW)
                    with act.Fori(0, further) as k:
                        act.wait_ge(tx.score, before + k + 1)
                        act.activation(fade_x[:, :], drop[:, :], ACT.Exp)
                        act.activation(weight[:, :], score[:, :], ACT.Exp).then_inc(tx.w, 1)
            act.wait_ge(s_tab, 1)
            groups(act, weights)
            act.wait_ge(e0.free, GROUPS + SLOTS)

            def sums(c, u):
                act.activation(colv[:, u, :], acc[:, columns(c)], ACT.Copy).then_inc(m_col, 1)

            def tanh(c, u):
                act.wait_ge(m_u, c + 1)
                act.activation(rowu[:, u, :], rowu[:, u, :], ACT.Tanh).then_inc(m_th, 1)

            def turned1(c, u):
                act.wait_ge(m_x1t, c + 1)
                act.activation(colw[0:D, u, :], bank[2 + u][0:D, :], ACT.Copy).then_inc(m_colw, 1)
                act.activation(acc[0:D, columns(c)], bank[2 + u][0:D, :], ACT.Copy)

            def gelu(c, u):
                act.wait_ge(m_h, c + 1)
                act.wait_ge(m_free, c + 1)
                act.activation(rowt[:, u, 0:CB * D], bank[4 + u][:, 0:CB * D], ACT.Gelu).then_inc(m_g, 1)

            sums(0, 0)
            tanh(0, 0)
            with act.Fori(0, CHUNKS // 2) as it:
                for u in range(2):
                    c = it * 2 + u
                    sums(c + 1, 1 - u)
                    turned1(c, u)
                    tanh(c + 1, 1 - u)
                    gelu(c, u)
            turned1(CHUNKS - 1, 0)
            gelu(CHUNKS - 1, 0)

            def mlp(c, u):
                act.wait_ge(f_y1, c + 1)
                act.activation(colw[0:D, u, :], bank[u][0:D, :], ACT.Gelu, bias=b1s[:, 0:1]).then_inc(f_g1, 1)
                act.wait_ge(f_y2, c + 1)
                act.activation(colv[0:D, u, :], bank[2 + u][0:D, :], ACT.Gelu, bias=b2s[:, 0:1]).then_inc(f_g2, 1)
            with act.Fori(0, CHUNKS // 2) as it:
                for u in range(2):
                    mlp(it * 2 + u, u)
            mlp(CHUNKS - 1, 0)

        @block.tensor
        def _(pe):
            pe.wait_ge(s_w, 16 * 10)
            pe.wait_ge(s_const, 4)
            pe.wait_ge(s_fill, 2)
            pe.transpose(bank[7][0:D, 0:D], w0x[0:D, 0:D], ident[0:D, 0:D]).then_inc(s_prep, 1)
            pe.wait_ge(s_prepc, 1)
            pe.matmul(bank[7][0:D, 128:130], w0t[:, :], att[:, :], start=True, stop=True).then_inc(s_prep, 1)
            pe.wait_ge(s_prepc, 2)

            def turn(c, u):
                pe.wait_ge(a_x, c + 1)
                for b in range(CB):
                    last = pe.transpose(bank[u][0:D, b * P:(b + 1) * P], xs[:, u, b * D:(b + 1) * D], ident[:, :])
                last.then_inc(a_t, 1)

            def project(c, u):
                pe.wait_ge(a_tc, c + 1)
                for b in range(CB):
                    last = pe.matmul(bank[2 + u][:, b * D2:(b + 1) * D2], colw[:, u, b * P:(b + 1) * P], w0x[:, :],
                                     start=True, stop=True)
                last.then_inc(a_row, 1)
                pe.wait_ge(a_peak, c + 1)
                pe.matmul(bank[4][0:D1, :], w0x[:, 0:D1], colw[:, u, :], start=True, stop=True)
                pe.matmul(bank[5][:, :], w0dst[:, :], colw[0:D, u, :], start=True, stop=True)
                pe.matmul(bank[6][:, :], w0both[:, :], colw[0:D, u, :], start=True, stop=True).then_inc(a_col, 1)
            chunks(pe, turn, project)

            pe.wait_ge(s_tab0, 1)
            for k in range(2):
                pe.matmul(bank[7][0:1, k * TG:(k + 1) * TG], low[:, k:k + 1], ident[0:TG, 0:TG], start=True, stop=True)
                last = pe.matmul(bank[7][0:1, GROUPS + k * TG:GROUPS + (k + 1) * TG], extra[:, k:k + 1],
                                 ident[0:TG, 0:TG], start=True, stop=True)
            last.then_inc(s_line, 1)

            pe.wait_ge(a_rowc, CHUNKS)
            pe.wait_ge(a_peak, CHUNKS + 1)
            pe.matmul(p_acc0, zeros[:, 0:D1], zeros[:, 0:WIN], start=True, stop=True).then_inc(e0.acc, 1)
            pe.wait_ge(s_tab, 1)

            def window0(t, top, topb, total, n, u, counted):
                pe.wait_ge(t.top, n)
                pe.transpose(top, peaks[:, :], ident[:, :]).then_inc(t.topt, 1)
                pe.wait_ge(t.diag, n)
                pe.matmul(topb, ones[0:WIN, :], top_diag[:, :], start=True, stop=True).then_inc(t.topb, 1)
                pe.wait_ge(t.w, n)
                for j in range(TILES):
                    last = pe.matmul(total, rows0(u)[:, j, 0:D1], by_tile(weight[:, :])[:, j, :],
                                     start=j == 0, stop=j == TILES - 1)
                last.then_inc(counted, 1)

            def attend(g, it, u):
                window0(t0, p_top, p_topb, p_acc0, g + 1, u, e0.acc)
                further = pe.value_load(win_tab[0:1, 1, bass.ds(g, 1)], min_val=0, max_val=MAXW)
                with pe.If(further > 0):
                    before = pe.value_load(win_tab[0:1, 2, bass.ds(g, 1)], min_val=0, max_val=GROUPS * MAXW)
                    with pe.Fori(0, further) as k:
                        window0(tx, px_top, px_topb, px_acc0, before + k + 1, u, x0_acc)
            peaks = top
            groups(pe, attend)

            def sums(c, u):
                pe.wait_ge(m_col, c + 1)
                for b in range(CB):
                    last = pe.transpose(bank[u][:, b * D1:(b + 1) * D1], colv[:, u, b * P:(b + 1) * P],
                                        ident[0:D1, 0:D1])
                last.then_inc(m_t, 1)

            def second(c, u):
                pe.wait_ge(m_x1, c + 1)
                for b in range(CB):
                    last = pe.transpose(bank[2 + u][0:D, b * P:(b + 1) * P], xs[:, u, b * D:(b + 1) * D], ident[:, :])
                last.then_inc(m_x1t, 1)
                pe.wait_ge(m_colw, c + 1)
                for b in range(CB):
                    last = pe.matmul(bank[4 + u][:, b * D:(b + 1) * D], colw[:, u, b * P:(b + 1) * P], w_prex[:, :],
                                     start=True, stop=True)
                last.then_inc(m_h, 1)
            chunks(pe, sums, second)

            pe.wait_ge(m_g, CHUNKS)
            pe.matmul(p_acc1[SLOTS - 1], zeros[:, 0:D], zeros[:, 0:WIN], start=True, stop=True).then_inc(e1.acc, 1)

            def window1(total, hot, u, counted):
                for j in range(TILES):
                    last = pe.matmul(total, rows1(u)[:, j, :], by_tile(hot)[:, j, :],
                                     start=j == 0, stop=j == TILES - 1)
                last.then_inc(counted, 1)

            def gather_sum(g, it, u):
                pe.wait_ge(e1_hot, g + 1)
                pe.wait_ge(e1_msg, g + 1)
                window1(p_acc1[u], onehot[:, u, :], u, e1.acc)
                further = pe.value_load(win_tab[0:1, 1, bass.ds(g, 1)], min_val=0, max_val=MAXW)
                with pe.If(further > 0):
                    before = pe.value_load(win_tab[0:1, 2, bass.ds(g, 1)], min_val=0, max_val=GROUPS * MAXW)
                    with pe.Fori(0, further) as k:
                        pe.wait_ge(x1_hot, before + k + 1)
                        window1(px_acc1, onehot_x[:, :], u, x1_acc)
            groups(pe, gather_sum)

            pe.wait_ge(e1.free, GROUPS + SLOTS)

            def hidden(c, u):
                pe.matmul(bank[u][0:D, :], w1s[:, :], acc[0:D, columns(c)], start=True, stop=True).then_inc(f_y1, 1)

            def output(c, u):
                pe.wait_ge(f_g1, c + 1)
                pe.matmul(bank[2 + u][0:D, :], w2s[:, :], colw[0:D, u, :], start=True, stop=True).then_inc(f_y2, 1)

            def back(c, u):
                pe.wait_ge(f_s, c + 1)
                for b in range(CB):
                    last = pe.transpose(bank[4 + u][:, b * D:(b + 1) * D], colv[0:D, u, b * P:(b + 1) * P],
                                        ident[0:D, 0:D])
                last.then_inc(f_t, 1)
            hidden(0, 0)
            output(0, 0)
            with pe.Fori(0, CHUNKS // 2) as it:
                for u in range(2):
                    c = it * 2 + u
                    hidden(c + 1, 1 - u)
                    back(c, u)
                    output(c + 1, 1 - u)
            back(CHUNKS - 1, 0)

        @block.vector
        def _(v):
            v.memset(x1[:, N // P:NP // P, :], 0.0).then_inc(s_fill, 1)
            v.memset(ones[:, :], 1.0)
            v.memset(run[:, :], 1.0)
            v.memset(zeros[:, :], 0.0)
            v.memset(fade[:, :], 1.0)
            v.memset(colw[D:D1, :, :], 1.0)
            v.memset(w0x[D:D1, :], 0.0).then_inc(s_v, 1)
            v.wait_ge(s_v, 1)
            v.memset(w0x[D:D1, D:D1], 1.0)
            v.memset(w0x[0:D, D:D1], 0.0).then_inc(s_fill, 1)

            v.wait_ge(s_prep, 1)
            v.tensor_copy(w0t[:, :], bank[7][0:D, 0:D]).then_inc(s_prepc, 1)
            v.wait_ge(s_prep, 2)
            v.tensor_copy(w0x[0:D, D1:D2], bank[7][0:D, 128:129])
            v.tensor_copy(w0att[:, :], bank[7][0:D, 128:130]).then_inc(s_v, 1)
            v.wait_ge(s_v, 2)
            v.tensor_scalar(w0dst[:, :], ones[0:D, :], w0att[:, 1:2], None, ALU.mult)
            v.tensor_scalar(w0both[:, :], ones[0:D, :], w0att[:, 0:1], w0att[:, 1:2], ALU.mult, ALU.add)\
                .then_inc(s_prepc, 1)

            v.wait_ge(s_x, 32)
            v.sem_inc(a_peak, 1)

            def stage(c, u):
                v.tensor_copy(by_block(xs[:, u, :]), x1[:, bass.ds(c * CB, CB), :]).then_inc(a_x, 1)

            def copy_out(c, u):
                v.wait_ge(a_row, c + 1)
                v.wait_ge(a_free, c + 1)
                v.tensor_copy(rowt[:, u, :], bank[2 + u][:, 0:CB * D2]).then_inc(a_rowc, 1)
                v.wait_ge(a_colc, c + 1)
                v.tensor_tensor(peak[:, columns(c)], bank[6][:, :], zcol[:, u, :], ALU.max).then_inc(a_peak, 1)
            chunks(v, stage, copy_out)

            v.wait_ge(s_dsts, 64)
            v.wait_ge(s_const, 4)
            v.tensor_reduce(low[:, :], dsts[:, :, :], AX.X, ALU.min)
            v.tensor_reduce(high[:, :], dsts[:, :, :], AX.X, ALU.max).then_inc(s_v, 1)
            v.wait_ge(s_v, 3)
            v.tensor_tensor(high[:, :], high[:, :], low[:, :], ALU.subtract).then_inc(s_v, 1)
            v.wait_ge(s_v, 4)
            v.tensor_tensor(more[:, :, :], high[:, :, None].broadcast_to([TG, 2, MAXW]),
                            steps_i[:, None, :].broadcast_to([TG, 2, MAXW]), ALU.is_ge).then_inc(s_v, 1)
            v.wait_ge(s_v, 5)
            v.tensor_reduce(extra[:, :], more[:, :, :], AX.X, ALU.add).then_inc(s_tab0, 1)
            v.wait_ge(s_line, 1)
            v.tensor_copy(line[:, :, :].rearrange("p a g -> p (a g)"), bank[7][0:1, 0:2 * GROUPS]).then_inc(s_v, 1)
            v.wait_ge(s_v, 6)
            v.tensor_copy(win_tab[:, 0:2, :], line[:, :, :])
            v.tensor_tensor_scan(upto[:, :], run[:, :], line[:, 1, :], 0.0, ALU.mult, ALU.add).then_inc(s_v, 1)
            v.wait_ge(s_v, 7)
            v.tensor_tensor(win_tab[:, 2, :], upto[:, :], line[:, 1, :], ALU.subtract).then_inc(s_tab, 1)
            v.wait_ge(s_tab, 1)

            v.wait_ge(a_peak, CHUNKS + 1)
            v.sem_inc(e0.free, SLOTS - 1)
            v.sem_inc(e1.free, SLOTS - 1)
            prev_reg = v.alloc_register("prev_window")
            lo_reg = v.alloc_register("window")
            further_reg = v.alloc_register("further")
            at_reg = v.alloc_register("at_window")

            def load_window(g):
                return (v.value_load(win_tab[0:1, 0, bass.ds(g, 1)], min_val=0, max_val=N - 1),
                        v.value_load(win_tab[0:1, 1, bass.ds(g, 1)], min_val=0, max_val=MAXW))

            def set_window(before, now):
                v.reg_mov(prev_reg, before)
                v.reg_mov(lo_reg, now[0])
                v.reg_mov(further_reg, now[1])

            def window():
                return (v.snap(lo_reg, min_val=0, max_val=N - 1), v.snap(further_reg, min_val=0, max_val=MAXW),
                        v.snap(prev_reg, min_val=0, max_val=N - 1))

            def scores(st, lo, u, wait_rows):
                st.link(v.tensor_tensor(by_tile(other[:, :]), over_window(dst_i[:, u, :]),
                                        over_tiles(iota[:, bass.ds(lo, WIN)]), ALU.not_equal))
                if wait_rows:
                    wait_rows()
                st.link(v.scalar_tensor_tensor(by_tile(other[:, :]), by_tile(other[:, :]), NEG,
                                               over_window(rows0(u)[:, :, D1]), ALU.mult, ALU.add))

            def largest(t):
                v.tensor_reduce(top[:, :], other[:, :].rearrange("p (j n) -> p n j", j=TILES), AX.X, ALU.max)\
                    .then_inc(t.top, 1)

            def shift(st, lo):
                st.step(v.tensor_tensor(by_tile(score[:, :]), by_tile(other[:, :]),
                                        over_tiles(adst[:, bass.ds(lo, WIN)]), ALU.add))

            def new_peak(st, t, n, lo, p_top_, p_topb_, between=None, ahead=None):
                here = bass.ds(lo, WIN)
                v.wait_ge(t.topt, n)
                st.step(v.tensor_reduce(top_col[:, :], p_top_, AX.X, ALU.max))
                column = st.n
                if between:
                    between()
                st.wait(column)
                v.tensor_scalar(top_diag[:, :], ident[0:WIN, 0:WIN], top_col[:, 0:1], None, ALU.mult)\
                    .then_inc(t.diag, 1)
                v.scalar_tensor_tensor(score[:, :], score[:, :], SLOPE, score[:, :], ALU.mult, ALU.max)
                v.wait_ge(t.topb, n)
                st.link(v.tensor_tensor(cand[:, :], p_topb_, adst[:, here], ALU.add))
                st.link(v.scalar_tensor_tensor(cand[:, :], cand[:, :], SLOPE, cand[:, :], ALU.mult, ALU.max))
                st.link(v.tensor_tensor(newp[:, :], cand[:, :], peak[:, here], ALU.max))
                st.step(v.tensor_tensor(drop[:, :], peak[0:D1, here], newp[0:D1, :], ALU.subtract))
                v.tensor_tensor(by_tile(score[:, :]), by_tile(score[:, :]), over_tiles(newp[:, :]), ALU.subtract)\
                    .then_inc(t.score, 1)
                got = ahead() if ahead else None
                st.wait()
                st.step(v.tensor_tensor(peak[:, here], cand[:, :], peak[:, here], ALU.max))
                return got

            def pad_last(e):
                v.memset(dst_i[:, 0, :], -1).then_inc(e.pad, 1)

            STEPS0 = 10
            STEPSX = 11

            def attend(g, it, u):
                lo, further, prev = window()
                if g is LAST:
                    pad_last(e0)
                st = Steps(v, e0.v, g * STEPS0, STEPS0)
                v.wait_ge(e0.dst[u], 16 * (it + 1))
                scores(st, lo, u, lambda: v.wait_ge(e0.rows[u], 16 * TILES * (it + 1)))
                largest(t0)
                before_here = bass.ds(prev, WIN)
                v.wait_ge(e0.acc, g + 1)
                shift(st, lo)
                st.step(v.tensor_tensor(acc[:, before_here], acc[:, before_here], fade[:, :], ALU.mult))
                faded = st.n

                def add_before():
                    st.wait(faded)
                    v.tensor_tensor(acc[:, before_here], acc[:, before_here], p_acc0, ALU.add).then_inc(e0.free, 1)
                after = new_peak(st, t0, g + 1, lo, p_top, p_topb, add_before,
                                 None if g is LAST else lambda: load_window(g + 1))
                st.done()
                with v.If(further > 0):
                    before = v.value_load(win_tab[0:1, 2, bass.ds(g, 1)], min_val=0, max_val=GROUPS * MAXW)
                    v.reg_mov(at_reg, lo)
                    with v.Fori(0, further) as k:
                        v.wait_ge(e0.acc, g + 2)
                        v.reg_add(at_reg, at_reg, WIN)
                        at = v.snap(at_reg, min_val=0, max_val=N - 1)
                        n = v.snap(before + k, min_val=0, max_val=GROUPS * MAXW)
                        sx = Steps(v, x0_v, n * STEPSX, STEPSX)
                        scores(sx, at, u, None)
                        largest(tx)
                        shift(sx, at)
                        new_peak(sx, tx, n + 1, at, px_top, px_topb)
                        v.wait_ge(x0_acc, n + 1)
                        sx.link(v.tensor_tensor(acc[:, bass.ds(at, WIN)], acc[:, bass.ds(at, WIN)], fade_x[:, :], ALU.mult))
                        sx.link(v.tensor_tensor(acc[:, bass.ds(at, WIN)], acc[:, bass.ds(at, WIN)], px_acc0, ALU.add))
                        sx.done()
                if g is not LAST:
                    set_window(lo, after)
                return lo

            set_window(0, load_window(0))
            prev = groups(v, attend)
            v.wait_ge(e0.acc, GROUPS + 1)
            v.tensor_tensor(acc[:, bass.ds(prev, WIN)], acc[:, bass.ds(prev, WIN)], fade[:, :], ALU.mult).then_inc(s_v, 1)
            v.wait_ge(s_v, 8)
            v.tensor_tensor(acc[:, bass.ds(prev, WIN)], acc[:, bass.ds(prev, WIN)], p_acc0, ALU.add).then_inc(e0.free, 1)

            def norm(st, y, made, var_made, rstd_made, n):
                total, mean, var, rstd = (stat[:, k, :] for k in range(4))
                st.link(v.tensor_reduce(total, y, AX.X, ALU.add))
                st.link(v.tensor_scalar(mean, total, 1.0 / D, None, ALU.mult))
                st.link(v.tensor_tensor(y, y, over_rows(mean), ALU.subtract))
                st.link(v.tensor_tensor(by_block(sq[:, :]), y, y, ALU.mult))
                st.link(v.tensor_reduce(var, by_block(sq[:, :]), AX.X, ALU.add))
                v.tensor_scalar(var, var, 1.0 / D, EPS, ALU.mult, ALU.add).then_inc(var_made, 1)
                v.wait_ge(rstd_made, n)
                return v.tensor_tensor(made, y, over_rows(rstd), ALU.mult)

            STEPSA, STEPSB = 3, 6
            def attended(c, u):
                st = Steps(v, m_va, c * STEPSA, STEPSA)
                v.wait_ge(m_t, c + 1)
                t = by_block(bank[u][:, :], D1)
                den = stat_d[:, 0, :]
                st.link(v.tensor_scalar(den, t[:, :, D], 1e-16, None, ALU.add))
                st.link(v.reciprocal(stat_d[:, 1, :], den))
                st.link(v.tensor_tensor(by_block(rowu[:, u, :]), t[:, :, 0:D], over_rows(stat_d[:, 1, :]), ALU.mult))
                v.tensor_tensor(by_block(rowu[:, u, :]), by_block(rowu[:, u, :]),
                                bias_b[:, None, :].broadcast_to([P, CB, D]), ALU.add).then_inc(m_u, 1)
                st.done()

            def norm1(c, u):
                st = Steps(v, m_v, c * STEPSB, STEPSB)
                v.wait_ge(m_th, c + 1)
                v.wait_ge(m_x1c, c + 1)
                y = by_block(rowu[:, u, :])
                st.link(v.tensor_tensor(y, y, x1[:, bass.ds(c * CB, CB), :], ALU.add))
                norm(st, y, by_block(xs[:, u, :]), m_var, m_rstd, c + 1).then_inc(m_x1, 1)
                st.done()
            chunks(v, attended, norm1)

            STEPS1 = 0

            def message(g, it, u):
                lo, further, prev = window()
                if g is LAST:
                    pad_last(e1)
                v.wait_ge(e1.dst[u], 16 * (it + 1))
                v.tensor_tensor(by_tile(onehot[:, u, :]), over_window(dst_i[:, u, :]),
                                over_tiles(iota[:, bass.ds(lo, WIN)]), ALU.is_equal).then_inc(e1_hot, 1)
                v.wait_ge(e1.rows[u], 16 * TILES * (it + 1))
                v.wait_ge(e1.attr[u], 16 * (it + 1))
                v.tensor_tensor(rows[:, u, 0:TILES * D], rows[:, u, 0:TILES * D], attr[:, u, :], ALU.mult)\
                    .then_inc(e1_msg, 1)
                v.wait_ge(e1.free, g + SLOTS - 1)
                v.wait_ge(e1.acc, g + 1)
                here = bass.ds(prev, WIN)
                v.tensor_tensor(acc[0:D, here], acc[0:D, here], p_acc1[(u - 1) % SLOTS], ALU.add).then_inc(e1.free, 1)
                after = None if g is LAST else load_window(g + 1)
                with v.If(further > 0):
                    before = v.value_load(win_tab[0:1, 2, bass.ds(g, 1)], min_val=0, max_val=GROUPS * MAXW)
                    v.reg_mov(at_reg, lo)
                    with v.Fori(0, further) as k:
                        v.reg_add(at_reg, at_reg, WIN)
                        at = v.snap(at_reg, min_val=0, max_val=N - 1)
                        v.tensor_tensor(by_tile(onehot_x[:, :]), over_window(dst_i[:, u, :]),
                                        over_tiles(iota[:, bass.ds(at, WIN)]), ALU.is_equal).then_inc(x1_hot, 1)
                        v.wait_ge(x1_acc, before + k + 1)
                        v.wait_ge(e1.free, g + SLOTS)
                        v.tensor_tensor(acc[0:D, bass.ds(at, WIN)], acc[0:D, bass.ds(at, WIN)], px_acc1, ALU.add)\
                            .then_inc(x1_v, 1)
                        v.wait_ge(x1_v, before + k + 1)
                if g is not LAST:
                    set_window(lo, after)
                return lo

            set_window(0, load_window(0))
            v.wait_ge(m_g, CHUNKS)
            prev = groups(v, message)
            v.wait_ge(e1.acc, GROUPS + 1)
            v.wait_ge(e1.free, GROUPS + SLOTS - 1)
            v.tensor_tensor(acc[0:D, bass.ds(prev, WIN)], acc[0:D, bass.ds(prev, WIN)], p_acc1[0], ALU.add)\
                .then_inc(e1.free, 1)
            v.wait_ge(e1.free, GROUPS + SLOTS)

            STEPSF = 6
            def last(c, u):
                v.wait_ge(f_g2, c + 1)
                v.tensor_tensor(colv[0:D, u, :], colv[0:D, u, :], acc[0:D, columns(c)], ALU.add).then_inc(f_s, 1)
                st = Steps(v, f_v, c * STEPSF, STEPSF)
                v.wait_ge(f_t, c + 1)
                v.wait_ge(f_free, c + 1)
                y = by_block(rowu[:, u, :])
                st.link(v.tensor_tensor(y, by_block(bank[4 + u][:, :]), x1[:, bass.ds(c * CB, CB), :], ALU.add))
                norm(st, y, by_block(rowt[:, u, :]), f_var, f_rstd, c + 1).then_inc(f_o, 1)
                st.done()
            chunks(v, None, last)


_INS = ['x', 'src', 'dst', 'edge_attr_96', 'L0_gnn_W', 'L0_gnn_att_src', 'L0_gnn_att_dst', 'L0_gnn_bias',
        'L1_gnn_W_pre', 'L1_gnn_b_pre', 'L1_gnn_W1', 'L1_gnn_b1', 'L1_gnn_W2', 'L1_gnn_b2']


def kernel(**inputs):
    import numpy as _np
    import concourse.bacc as _bacc
    from concourse import mybir as _mybir
    from concourse.bass_utils import run_bass_kernel_spmd as _run

    nc = _bacc.Bacc("TRN2", target_bir_lowering=False, num_devices=1)
    arrays, args = {}, []
    for name in _INS:
        a = _np.ascontiguousarray(inputs[name])
        arrays[f"in_{name}_dram"] = a
        args.append(nc.dram_tensor(f"in_{name}_dram", a.shape, _mybir.dt.from_np(a.dtype), kind="ExternalInput").ap())
    shape = inputs['x'].shape
    args.append(nc.dram_tensor("out_0_dram", shape, _mybir.dt.float32, kind="ExternalOutput").ap())
    gnn(nc, *args)
    r = _run(nc, [arrays], core_ids=[0])
    return r.results[0]["out_0_dram"]
```

```python
from contextlib import ExitStack

import concourse.bass as bass
from concourse import mybir

FP32 = mybir.dt.float32
INT32 = mybir.dt.int32
ALU = mybir.AluOpType
ACT = mybir.ActivationFunctionType
AX = mybir.AxisListType

P = 128
TILES = 8
SLOTS = 5
RING = 3
WIN = 72
NEG = -1e30
SLOPE = 0.2
EPS = 1e-5
CB = 4


def gnn(nc, x, src, dst, edge_attr, w0, att_src, att_dst, bias0, w_pre, b_pre, w1, b1, w2, b2, out):
    N, D = x.shape
    E = src.shape[0]
    GE = P * TILES
    GROUPS = -(-E // GE)
    ROUNDS = (GROUPS - 1) // SLOTS
    LAST = GROUPS - 1
    LAST_P = (E - LAST * GE) // TILES
    assert LAST == ROUNDS * SLOTS and LAST_P * TILES == E - LAST * GE
    D1 = D + 1
    D2 = D + 2
    CN = CB * P
    CHUNKS = -(-N // CN)
    LAST_N = N - (CHUNKS - 1) * CN
    assert LAST_N <= P and CHUNKS % RING == 1
    FULL = N // P
    NP = CHUNKS * CN
    assert NP >= N + WIN
    TG = GROUPS // 2
    assert GROUPS == 2 * TG and TG <= P
    MAXW = -(-(N - 1) // WIN)

    ctx = ExitStack()
    with ctx:
        def sb(name, shape, dt=FP32):
            return ctx.enter_context(nc.sbuf_tensor(name, shape, dt))

        def sem(name):
            return ctx.enter_context(nc.semaphore(name))

        def sems(name, n):
            return [sem(f"{name}{i}") for i in range(n)]

        table0 = nc.dram_tensor("table0", (N, D2), FP32, kind="Internal").ap()
        table1 = nc.dram_tensor("table1", (N, D), FP32, kind="Internal").ap()

        iota = sb("iota", [P, NP], mybir.dt.int16)
        adst = sb("adst", [P, NP])
        peak = sb("peak", [P, NP])
        acc = sb("acc", [D1, NP])
        x1 = sb("x1", [P, NP // P, D])

        src_i = sb("src_i", [P, SLOTS, TILES], INT32)
        dst_i = sb("dst_i", [P, SLOTS, TILES], INT32)
        rows = sb("rows", [P, SLOTS, TILES * D2])
        attr = sb("attr", [P, SLOTS, TILES * D])
        onehot = sb("onehot", [P, SLOTS, TILES * WIN])

        other = sb("other", [P, TILES * WIN])
        score = sb("score", [P, TILES * WIN])
        weight = sb("weight", [P, TILES * WIN])
        top = sb("top", [P, WIN])
        top_col = sb("top_col", [WIN, 1])
        top_diag = sb("top_diag", [WIN, WIN])
        cand = sb("cand", [P, WIN])
        newp = sb("newp", [P, WIN])
        drop = sb("drop", [D1, WIN])
        fade = sb("fade", [D1, WIN])
        fade_x = sb("fade_x", [D1, WIN])
        onehot_x = sb("onehot_x", [P, TILES * WIN])

        ident = sb("ident", [P, P])
        ones = sb("ones", [P, P])
        zeros = sb("zeros", [P, P])
        w0x = sb("w0x", [D1, D2])
        w0t = sb("w0t", [D, D])
        att = sb("att", [D, 2])
        w0att = sb("w0att", [D, 2])
        w0dst = sb("w0dst", [D, P])
        w0both = sb("w0both", [D, P])
        turn_b = sb("turn_b", [D1, D1])
        w_prex = sb("w_prex", [D1, D])
        w1s = sb("w1s", [D, D])
        w2s = sb("w2s", [D, D])
        b1s = sb("b1s", [D, 1])
        b2s = sb("b2s", [D, 1])

        xs = sb("xs", [P, RING, CB * D])
        colw = sb("colw", [D1, RING, CN])
        colv = sb("colv", [D1, RING, CN])
        zcol = sb("zcol", [P, RING, CN])
        rowt = sb("rowt", [P, RING, CB * D2])
        rowu = sb("rowu", [P, RING, CB * D])
        den = sb("den", [P, RING, CB])
        rden = sb("rden", [P, RING, CB])
        bst = sb("bst", [P, CB, 6])
        mv = sb("mv", [P, RING, 2 * CB])
        var = sb("var", [P, RING, CB])
        rstd = sb("rstd", [P, RING, CB])
        minus_half = sb("minus_half", [P, CB])

        dsts = attr[0:TG, :, :].rearrange("p s n -> p (s n)")[:, 0:2 * GE].bitcast(INT32)\
            .rearrange("p (k e) -> p k e", k=2)
        low = sb("low", [TG, 2])
        high = sb("high", [TG, 2])
        steps_i = sb("steps_i", [TG, MAXW], INT32)
        more = sb("more", [TG, 2, MAXW])
        extra = sb("extra", [TG, 2])
        line = sb("line", [1, 2, GROUPS])
        upto = sb("upto", [1, GROUPS])
        run = sb("run", [1, GROUPS])
        win_tab = sb("win_tab", [1, 3, GROUPS], INT32)

        bank = [ctx.enter_context(nc.psum_tensor(f"bank{i}", [P, 512], FP32)) for i in range(8)]

        s_xa = sem("s_xa")
        s_xb = sem("s_xb")
        s_w0 = sem("s_w0")
        s_w = sem("s_w")
        s_turn = sem("s_turn")
        s_bias = sem("s_bias")
        s_dsts = sem("s_dsts")
        s_const = sem("s_const")
        s_fill = sem("s_fill")
        s_prep = sem("s_prep")
        s_prepc = sem("s_prepc")
        s_line = sem("s_line")
        s_tab0 = sem("s_tab0")
        s_tab = sem("s_tab")
        s_mark = sem("s_mark")
        s_v = sem("s_v")

        a_x = sem("a_x")
        a_t = sem("a_t")
        a_tc = sem("a_tc")
        a_row = sem("a_row")
        a_rowc = sem("a_rowc")
        a_keep = sem("a_keep")
        a_st = sems("a_st", RING)
        a_free = sem("a_free")
        a_h = sem("a_h")
        a_hc = sem("a_hc")
        a_col = sem("a_col")
        a_colc = sem("a_colc")
        a_peak = sem("a_peak")
        m_col = sem("m_col")
        m_t = sem("m_t")
        m_rden = sem("m_rden")
        m_th = sem("m_th")
        m_var = sem("m_var")
        m_rstd = sem("m_rstd")
        m_x1 = sem("m_x1")
        m_kept = sem("m_kept")
        m_x1t = sem("m_x1t")
        m_colw = sem("m_colw")
        m_kc = sem("m_kc")
        m_h = sem("m_h")
        m_g = sem("m_g")
        m_st = sems("m_st", RING)
        m_free = sem("m_free")
        m_v, m_vd = sem("m_v"), sem("m_vd")
        f_y1 = sem("f_y1")
        f_g1 = sem("f_g1")
        f_y2 = sem("f_y2")
        f_g2 = sem("f_g2")
        f_s = sem("f_s")
        f_t = sem("f_t")
        f_var = sem("f_var")
        f_rstd = sem("f_rstd")
        f_o = sem("f_o")
        f_st = sems("f_st", RING)
        f_free = sem("f_free")
        f_v = sem("f_v")

        class Edge:
            def __init__(self, n):
                self.src = sems(f"e{n}_src", SLOTS)
                self.dst = sems(f"e{n}_dst", SLOTS)
                self.attr = sems(f"e{n}_attr", SLOTS)
                self.rows = sems(f"e{n}_rows", SLOTS)
                self.go = sem(f"e{n}_go")
                self.free = sem(f"e{n}_free")
                self.pad = sem(f"e{n}_pad")
                self.acc = sem(f"e{n}_acc")
                self.v = sem(f"e{n}_v")

        class Top:
            def __init__(self, n):
                self.top = sem(f"{n}_top")
                self.topt = sem(f"{n}_topt")
                self.diag = sem(f"{n}_diag")
                self.topb = sem(f"{n}_topb")
                self.score = sem(f"{n}_score")
                self.w = sem(f"{n}_w")

        e0, e1 = Edge(0), Edge(1)
        t0, tx = Top("t0"), Top("tx")
        x0_acc, x1_acc = sem("x0_acc"), sem("x1_acc")
        x0_v, x1_v = sem("x0_v"), sem("x1_v")
        e1_hot, e1_msg, x1_hot = sem("e1_hot"), sem("e1_msg"), sem("x1_hot")

        p_top, px_top = bank[0][0:WIN, 0:P], bank[3][0:WIN, 0:P]
        p_topb, px_topb = bank[1][:, 0:WIN], bank[4][:, 0:WIN]
        p_acc0, px_acc0 = bank[2][0:D1, 0:WIN], bank[5][0:D1, 0:WIN]
        p_acc1, px_acc1 = [bank[i][0:D, 0:WIN] for i in range(SLOTS)], bank[5][0:D, 0:WIN]
        assert SLOTS <= 5

        def by_tile(t):
            return t.rearrange("p (j n) -> p j n", j=TILES)

        def rows0(u):
            return rows[:, u, :].rearrange("p (j d) -> p j d", j=TILES)

        def rows1(u):
            return rows[:, u, 0:TILES * D].rearrange("p (j d) -> p j d", j=TILES)

        def over_tiles(t):
            return t[:, None, :].broadcast_to([P, TILES, WIN])

        def over_window(t):
            return t[:, :, None].broadcast_to([P, TILES, WIN])

        def by_block(t, w=D):
            return t[:, 0:CB * w].rearrange("p (b d) -> p b d", d=w)

        def columns(c):
            return bass.ds(c * CN, CN)

        def groups(eng, body):
            with eng.Fori(0, ROUNDS) as it:
                for u in range(SLOTS):
                    body(it * SLOTS + u, it, u)
            return body(LAST, ROUNDS, 0)

        def chunks(eng, *stages, enter=None):
            most = max(lead for lead, _ in stages)
            rounds = (CHUNKS - most) // RING

            def peeled(t):
                for lead, body in stages:
                    if 0 <= t + lead < CHUNKS:
                        body(t + lead, (t + lead) % RING)
            for t in range(-most, 0):
                peeled(t)
            if enter:
                enter()
            with eng.Fori(0, rounds) as it:
                for u in range(RING):
                    for lead, body in stages:
                        body(it * RING + (u + lead), (u + lead) % RING)
            for t in range(rounds * RING, CHUNKS):
                peeled(t)

        class Steps:
            def __init__(self, eng, s, base, most):
                self.eng, self.s, self.base, self.n, self.most = eng, s, base, 0, most

            def step(self, ins):
                self.n += 1
                assert self.n <= self.most
                ins.then_inc(self.s, 1)

            def wait(self, n=None):
                self.eng.wait_ge(self.s, self.base + (n or self.n))

            def link(self, ins):
                self.step(ins)
                self.wait()

            def done(self):
                assert self.n == self.most

        block = ctx.enter_context(nc.Block())

        @block.sync
        def _(sp):
            part = 2 * CB
            sp.dma_start(w0x[0:D, 0:D], w0).then_inc(s_w0, 16)
            sp.dma_start(att[:, 0:1], att_src.rearrange("(d a) -> d a", a=1)).then_inc(s_w0, 16)
            sp.dma_start(att[:, 1:2], att_dst.rearrange("(d a) -> d a", a=1)).then_inc(s_w0, 16)
            sp.dma_start(x1[:, 0:part, :], x[0:part * P, :].rearrange("(b p) d -> p b d", p=P)).then_inc(s_xa, 16)
            sp.wait_ge(s_fill, 1)
            sp.dma_start(x1[:, part:FULL, :], x[part * P:FULL * P, :].rearrange("(b p) d -> p b d", p=P))\
                .then_inc(s_xb, 16)
            sp.dma_start(x1[0:N - FULL * P, FULL, :], x[FULL * P:N, :]).then_inc(s_xb, 16)
            sp.dma_start(w_prex[0:D, :], w_pre).then_inc(s_w, 16)
            sp.dma_start(w_prex[D:D1, :], b_pre.rearrange("(a d) -> a d", a=1)).then_inc(s_w, 16)
            sp.dma_start(w1s[:, :], w1).then_inc(s_w, 16)
            sp.dma_start(w2s[:, :], w2).then_inc(s_w, 16)
            sp.dma_start(b1s[:, :], b1.rearrange("(d a) -> d a", a=1)).then_inc(s_w, 16)
            sp.dma_start(b2s[:, :], b2.rearrange("(d a) -> d a", a=1)).then_inc(s_w, 16)
            sp.wait_ge(s_turn, 1)
            sp.dma_start(turn_b[D:D1, 0:D], bias0.rearrange("(a d) -> a d", a=1)).then_inc(s_bias, 16)

            def stores(dram, w, made, stored, free):
                sp.sem_inc(free, RING)
                with sp.Fori(0, CHUNKS // RING) as it:
                    for u in range(RING):
                        c = it * RING + u
                        sp.wait_ge(made, c + 1)
                        sp.dma_start(dram[bass.ds(c * CN, CN), :].rearrange("(b p) d -> p b d", p=P),
                                     by_block(rowt[:, u, :], w)).then_inc(stored[u], 16)
                        sp.wait_ge(stored[u], 16 * (it + 1))
                        sp.sem_inc(free, 1)
                sp.wait_ge(made, CHUNKS)
                sp.dma_start(dram[(CHUNKS - 1) * CN:N, :], rowt[0:LAST_N, 0, 0:w]).then_inc(stored[0], 16)
                sp.wait_ge(stored[0], 16 * (CHUNKS // RING + 1))

            def load_edges(e, attrs):
                def body(g, it, u):
                    n = LAST_P * TILES if g is LAST else GE
                    m = n // TILES
                    sp.wait_ge(e.free, g + 1)
                    sp.dma_start(src_i[0:m, u, :], src[bass.ds(g * GE, n)].rearrange("(p j) -> p j", j=TILES))\
                        .then_inc(e.src[u], 16)
                    if g is LAST:
                        sp.wait_ge(e.pad, 1)
                    sp.dma_start(dst_i[0:m, u, :], dst[bass.ds(g * GE, n)].rearrange("(p j) -> p j", j=TILES))\
                        .then_inc(e.dst[u], 16)
                    if attrs:
                        sp.dma_start(attr[0:m, u, :],
                                     edge_attr[bass.ds(g * GE, n), :].rearrange("(p j) d -> p (j d)", j=TILES))\
                            .then_inc(e.attr[u], 16)
                return body

            stores(table0, D2, a_rowc, a_st, a_free)
            groups(sp, load_edges(e0, False))
            stores(table1, D, m_g, m_st, m_free)
            groups(sp, load_edges(e1, True))
            stores(out, D, f_o, f_st, f_free)

        @block.gpsimd
        def _(pool):
            pool.memset(ident[:, :], 0.0).then_inc(s_const, 1)
            pool.wait_ge(s_const, 1)
            pool.affine_select(out=ident[:, :], in_=ident[:, :], compare_op=ALU.not_equal, fill=1.0,
                               base=0, pattern=[[-1, P]], channel_multiplier=1).then_inc(s_const, 1)
            pool.memset(minus_half[:, :], -0.5)
            pool.iota(steps_i[:, :], pattern=[[WIN, MAXW]], base=WIN, channel_multiplier=0).then_inc(s_const, 1)
            pool.iota(iota[:, :], pattern=[[1, NP]], base=0, channel_multiplier=0).then_inc(s_const, 1)

            def gather(e, table, width):
                def body(g, it, u):
                    pool.wait_ge(e.src[u], 16 * (it + 1))
                    pool.sem_inc(e.go, 1)
                    for j in range(TILES):
                        pool.indirect_dma_start(rows[:, u, j * width:(j + 1) * width], None, table,
                                                bass.IndirectOffsetOnAxis(ap=src_i[:, u, j:j + 1], axis=0))\
                            .then_inc(e.rows[u], 16)
                return body

            def written(stored):
                pool.wait_ge(stored[0], 16 * (CHUNKS // RING + 1))
                for u in range(1, RING):
                    pool.wait_ge(stored[u], 16 * (CHUNKS // RING))

            written(a_st)
            groups(pool, gather(e0, table0, D2))

            def keep(c, u):
                pool.wait_ge(m_x1, c + 1)
                pool.tensor_copy(x1[:, bass.ds(c * CB, CB), :], by_block(xs[:, u, :])).then_inc(m_kept, 1)

            def power(made, given):
                def body(c, u):
                    pool.wait_ge(made, c + 1)
                    pool.tensor_tensor(rstd[:, u, :], var[:, u, :], minus_half[:, :], ALU.pow).then_inc(given, 1)
                return body
            chunks(pool, (0, keep), (1, power(m_var, m_rstd)))
            written(m_st)
            groups(pool, gather(e1, table1, D))

            chunks(pool, (0, power(f_var, f_rstd)))

        @block.scalar
        def _(act):
            act.dma_start(dsts[:, 0, :], dst[0:TG * GE].rearrange("(p e) -> p e", e=GE)).then_inc(s_dsts, 16)
            act.dma_start(dsts[0:TG - 1, 1, :], dst[TG * GE:LAST * GE].rearrange("(p e) -> p e", e=GE))\
                .then_inc(s_dsts, 16)
            tail = E - LAST * GE
            rep = 64
            assert (GE - tail) % rep == 0 and tail >= rep
            act.dma_start(dsts[TG - 1:TG, 1, 0:tail], dst[LAST * GE:E].rearrange("(p e) -> p e", p=1))\
                .then_inc(s_dsts, 16)
            act.dma_start(dsts[TG - 1:TG, 1, tail:GE].rearrange("p (a b) -> p a b", b=rep),
                          dst[E - rep:E].rearrange("(p a b) -> p a b", p=1, a=1)
                          .broadcast_to([1, (GE - tail) // rep, rep])).then_inc(s_dsts, 16)

            def turned(c, u):
                act.wait_ge(a_t, c + 1)
                act.activation(colw[0:D, u, :], bank[u][0:D, :], ACT.Copy).then_inc(a_tc, 1)

            def back_copied(c, u):
                act.wait_ge(a_h, c + 1)
                act.activation(acc[:, columns(c)], bank[3 + u][0:D1, :], ACT.Copy).then_inc(a_hc, 1)

            def columns0(c, u):
                act.wait_ge(a_col, c + 1)
                act.activation(adst[:, columns(c)], bank[u][:, :], ACT.Copy)
                act.activation(zcol[:, u, :], bank[3 + u][:, :], ACT.Copy, scale=SLOPE).then_inc(a_colc, 1)
            act.wait_ge(s_fill, 2)
            chunks(act, (2, turned), (0, back_copied))
            chunks(act, (0, columns0))

            def weights(g, it, u):
                act.wait_ge(t0.score, g + 1)
                act.activation(fade[:, :], drop[:, :], ACT.Exp)
                act.activation(weight[:, :], score[:, :], ACT.Exp).then_inc(t0.w, 1)
                further = act.value_load(win_tab[0:1, 1, bass.ds(g, 1)], min_val=0, max_val=MAXW)
                with act.If(further > 0):
                    before = act.value_load(win_tab[0:1, 2, bass.ds(g, 1)], min_val=0, max_val=GROUPS * MAXW)
                    with act.Fori(0, further) as k:
                        act.wait_ge(tx.score, before + k + 1)
                        act.activation(fade_x[:, :], drop[:, :], ACT.Exp)
                        act.activation(weight[:, :], score[:, :], ACT.Exp).then_inc(tx.w, 1)
            act.wait_ge(s_tab, 1)
            groups(act, weights)
            def tanh(c, u):
                act.wait_ge(m_rden, c + 1)
                for b in range(CB):
                    last = act.activation(rowu[:, u, b * D:(b + 1) * D], bank[u][:, b * D1:b * D1 + D], ACT.Tanh,
                                          scale=rden[:, u, b:b + 1])
                last.then_inc(m_th, 1)

            def turned1(c, u):
                act.wait_ge(m_x1t, c + 1)
                act.activation(colw[0:D, u, :], bank[3 + u][0:D, :], ACT.Copy).then_inc(m_colw, 1)

            def gelu(c, u):
                act.wait_ge(m_h, c + 1)
                act.wait_ge(m_free, c + 1)
                act.activation(rowt[:, u, 0:CB * D], bank[3 + u][:, 0:CB * D], ACT.Gelu).then_inc(m_g, 1)
            chunks(act, (0, gelu), (1, turned1), (3, tanh))

            def gelu1(c, u):
                act.wait_ge(f_y1, c + 1)
                act.activation(colw[0:D, u, :], bank[u][0:D, :], ACT.Gelu, bias=b1s[:, 0:1]).then_inc(f_g1, 1)

            def gelu2(c, u):
                act.wait_ge(f_y2, c + 1)
                act.activation(colv[0:D, u, :], bank[3 + u][0:D, :], ACT.Gelu, bias=b2s[:, 0:1]).then_inc(f_g2, 1)
            chunks(act, (1, gelu1), (0, gelu2))

        @block.tensor
        def _(pe):
            pe.wait_ge(s_w0, 16 * 3)
            pe.wait_ge(s_const, 4)
            pe.wait_ge(s_fill, 2)
            pe.transpose(bank[7][0:D, 0:D], w0x[0:D, 0:D], ident[0:D, 0:D]).then_inc(s_prep, 1)
            pe.wait_ge(s_prepc, 1)
            pe.matmul(bank[7][0:D, 128:130], w0t[:, :], att[:, :], start=True, stop=True).then_inc(s_prep, 1)
            pe.wait_ge(s_prepc, 2)

            def turn(c, u):
                pe.wait_ge(a_x, c + 1)
                for b in range(CB):
                    last = pe.transpose(bank[u][0:D, b * P:(b + 1) * P], xs[:, u, b * D:(b + 1) * D], ident[:, :])
                last.then_inc(a_t, 1)

            def project(c, u):
                pe.wait_ge(a_tc, c + 1)
                for b in range(CB):
                    last = pe.matmul(bank[3 + u][:, b * D2:(b + 1) * D2], colw[:, u, b * P:(b + 1) * P], w0x[:, :],
                                     start=True, stop=True)
                last.then_inc(a_row, 1)

            def turn_back(c, u):
                pe.wait_ge(a_rowc, c + 1)
                for b in range(CB):
                    last = pe.transpose(bank[3 + u][0:D1, b * P:(b + 1) * P],
                                        rowt[:, u, b * D2:b * D2 + D1], ident[:, :])
                last.then_inc(a_h, 1)
            chunks(pe, (2, turn), (1, project), (0, turn_back))

            pe.wait_ge(s_tab0, 1)
            for k in range(2):
                pe.matmul(bank[7][0:1, k * TG:(k + 1) * TG], low[:, k:k + 1], ident[0:TG, 0:TG], start=True, stop=True)
                last = pe.matmul(bank[7][0:1, GROUPS + k * TG:GROUPS + (k + 1) * TG], extra[:, k:k + 1],
                                 ident[0:TG, 0:TG], start=True, stop=True)
            last.then_inc(s_line, 1)

            def by_column(c, u):
                xt = peak[0:D, columns(c)]
                pe.wait_ge(a_peak, c + 1)
                pe.matmul(bank[u][:, :], w0dst[:, :], xt, start=True, stop=True)
                pe.matmul(bank[3 + u][:, :], w0both[:, :], xt, start=True, stop=True).then_inc(a_col, 1)
            pe.wait_ge(a_hc, CHUNKS)
            pe.wait_ge(a_keep, CHUNKS)
            chunks(pe, (0, by_column))

            pe.wait_ge(a_peak, CHUNKS + RING)
            pe.matmul(p_acc0, zeros[:, 0:D1], zeros[:, 0:WIN], start=True, stop=True).then_inc(e0.acc, 1)
            pe.wait_ge(s_tab, 1)

            def window0(t, top, topb, total, n, u, counted):
                pe.wait_ge(t.top, n)
                pe.transpose(top, peaks[:, :], ident[:, :]).then_inc(t.topt, 1)
                pe.wait_ge(t.diag, n)
                pe.matmul(topb, ones[0:WIN, :], top_diag[:, :], start=True, stop=True).then_inc(t.topb, 1)
                pe.wait_ge(t.w, n)
                for j in range(TILES):
                    last = pe.matmul(total, rows0(u)[:, j, 0:D1], by_tile(weight[:, :])[:, j, :],
                                     start=j == 0, stop=j == TILES - 1)
                last.then_inc(counted, 1)

            def attend(g, it, u):
                window0(t0, p_top, p_topb, p_acc0, g + 1, u, e0.acc)
                further = pe.value_load(win_tab[0:1, 1, bass.ds(g, 1)], min_val=0, max_val=MAXW)
                with pe.If(further > 0):
                    before = pe.value_load(win_tab[0:1, 2, bass.ds(g, 1)], min_val=0, max_val=GROUPS * MAXW)
                    with pe.Fori(0, further) as k:
                        window0(tx, px_top, px_topb, px_acc0, before + k + 1, u, x0_acc)
            peaks = top
            groups(pe, attend)

            pe.wait_ge(s_w, 16 * 6)
            pe.wait_ge(s_bias, 16)

            def sums(c, u):
                pe.wait_ge(m_col, c + 1)
                for b in range(CB):
                    last = pe.matmul(bank[u][:, b * D1:(b + 1) * D1], colv[:, u, b * P:(b + 1) * P], turn_b[:, :],
                                     start=True, stop=True)
                last.then_inc(m_t, 1)

            def turn1(c, u):
                pe.wait_ge(m_x1, c + 1)
                for b in range(CB):
                    last = pe.transpose(bank[3 + u][0:D, b * P:(b + 1) * P], xs[:, u, b * D:(b + 1) * D], ident[:, :])
                last.then_inc(m_x1t, 1)

            def project1(c, u):
                pe.wait_ge(m_colw, c + 1)
                for b in range(CB):
                    last = pe.matmul(bank[3 + u][:, b * D:(b + 1) * D], colw[:, u, b * P:(b + 1) * P], w_prex[:, :],
                                     start=True, stop=True)
                last.then_inc(m_h, 1)
            chunks(pe, (0, turn1), (3, sums), (0, project1))

            pe.wait_ge(m_g, CHUNKS)
            pe.matmul(p_acc1[SLOTS - 1], zeros[:, 0:D], zeros[:, 0:WIN], start=True, stop=True).then_inc(e1.acc, 1)

            def window1(total, hot, u, counted):
                for j in range(TILES):
                    last = pe.matmul(total, rows1(u)[:, j, :], by_tile(hot)[:, j, :],
                                     start=j == 0, stop=j == TILES - 1)
                last.then_inc(counted, 1)

            def gather_sum(g, it, u):
                pe.wait_ge(e1_hot, g + 1)
                pe.wait_ge(e1_msg, g + 1)
                window1(p_acc1[u], onehot[:, u, :], u, e1.acc)
                further = pe.value_load(win_tab[0:1, 1, bass.ds(g, 1)], min_val=0, max_val=MAXW)
                with pe.If(further > 0):
                    before = pe.value_load(win_tab[0:1, 2, bass.ds(g, 1)], min_val=0, max_val=GROUPS * MAXW)
                    with pe.Fori(0, further) as k:
                        pe.wait_ge(x1_hot, before + k + 1)
                        window1(px_acc1, onehot_x[:, :], u, x1_acc)
            groups(pe, gather_sum)

            pe.wait_ge(e1.free, GROUPS + SLOTS)

            def hidden(c, u):
                pe.matmul(bank[u][0:D, :], w1s[:, :], acc[0:D, columns(c)], start=True, stop=True).then_inc(f_y1, 1)

            def output(c, u):
                pe.wait_ge(f_g1, c + 1)
                pe.matmul(bank[3 + u][0:D, :], w2s[:, :], colw[0:D, u, :], start=True, stop=True).then_inc(f_y2, 1)

            def back(c, u):
                pe.wait_ge(f_s, c + 1)
                for b in range(CB):
                    last = pe.transpose(bank[3 + u][:, b * D:(b + 1) * D], colv[0:D, u, b * P:(b + 1) * P],
                                        ident[0:D, 0:D])
                last.then_inc(f_t, 1)
            chunks(pe, (0, back), (2, hidden), (1, output))

        @block.vector
        def _(v):
            v.sem_inc(e0.free, SLOTS - 1)
            v.sem_inc(e1.free, SLOTS - 1)
            v.memset(x1[:, N // P:NP // P, :], 0.0).then_inc(s_fill, 1)
            v.memset(ones[:, :], 1.0)
            v.memset(run[:, :], 1.0)
            v.memset(zeros[:, :], 0.0)
            v.memset(fade[:, :], 1.0)
            v.memset(colw[D:D1, :, :], 1.0)
            v.memset(w0x[D:D1, :], 0.0).then_inc(s_v, 1)
            v.wait_ge(s_v, 1)
            v.memset(w0x[D:D1, D:D1], 1.0)
            v.memset(w0x[0:D, D:D1], 0.0).then_inc(s_fill, 1)
            v.wait_ge(s_const, 2)
            v.tensor_copy(turn_b[:, :], ident[0:D1, 0:D1]).then_inc(s_turn, 1)

            v.wait_ge(s_prep, 1)
            v.tensor_copy(w0t[:, :], bank[7][0:D, 0:D]).then_inc(s_prepc, 1)
            v.wait_ge(s_prep, 2)
            v.tensor_copy(w0x[0:D, D1:D2], bank[7][0:D, 128:129])
            v.tensor_copy(w0att[:, :], bank[7][0:D, 128:130]).then_inc(s_v, 1)
            v.wait_ge(s_v, 2)
            v.tensor_scalar(w0dst[:, :], ones[0:D, :], w0att[:, 1:2], None, ALU.mult)
            v.tensor_scalar(w0both[:, :], ones[0:D, :], w0att[:, 0:1], w0att[:, 1:2], ALU.mult, ALU.add)\
                .then_inc(s_prepc, 1)

            v.wait_ge(s_xa, 16)

            def stage(c, u):
                v.tensor_copy(by_block(xs[:, u, :]), x1[:, bass.ds(c * CB, CB), :]).then_inc(a_x, 1)

            def keep_turned(c, u):
                v.wait_ge(a_tc, c + 1)
                v.tensor_copy(peak[0:D, columns(c)], colw[0:D, u, :]).then_inc(a_keep, 1)

            def copy_out(c, u):
                v.wait_ge(a_row, c + 1)
                v.wait_ge(a_free, c + 1)
                v.tensor_copy(rowt[:, u, :], bank[3 + u][:, 0:CB * D2]).then_inc(a_rowc, 1)
            chunks(v, (2, stage), (1, keep_turned), (0, copy_out), enter=lambda: v.wait_ge(s_xb, 32))
            v.sem_inc(a_peak, RING)

            v.wait_ge(s_dsts, 64)
            v.wait_ge(s_const, 4)
            v.tensor_reduce(low[:, :], dsts[:, :, :], AX.X, ALU.min)
            v.tensor_reduce(high[:, :], dsts[:, :, :], AX.X, ALU.max).then_inc(s_v, 1)
            v.wait_ge(s_v, 3)
            v.tensor_tensor(high[:, :], high[:, :], low[:, :], ALU.subtract).then_inc(s_v, 1)
            v.wait_ge(s_v, 4)
            v.tensor_tensor(more[:, :, :], high[:, :, None].broadcast_to([TG, 2, MAXW]),
                            steps_i[:, None, :].broadcast_to([TG, 2, MAXW]), ALU.is_ge).then_inc(s_v, 1)
            v.wait_ge(s_v, 5)
            v.tensor_reduce(extra[:, :], more[:, :, :], AX.X, ALU.add).then_inc(s_tab0, 1)
            v.wait_ge(s_line, 1)
            v.tensor_copy(line[:, :, :].rearrange("p a g -> p (a g)"), bank[7][0:1, 0:2 * GROUPS]).then_inc(s_v, 1)
            v.wait_ge(s_v, 6)
            v.tensor_copy(win_tab[:, 0:2, :], line[:, :, :])
            v.tensor_tensor_scan(upto[:, :], run[:, :], line[:, 1, :], 0.0, ALU.mult, ALU.add).then_inc(s_v, 1)
            v.wait_ge(s_v, 7)
            v.tensor_tensor(win_tab[:, 2, :], upto[:, :], line[:, 1, :], ALU.subtract).then_inc(s_tab, 1)
            v.wait_ge(s_tab, 1)

            def peaks(c, u):
                v.wait_ge(a_colc, c + 1)
                v.tensor_tensor(peak[:, columns(c)], bank[3 + u][:, :], zcol[:, u, :], ALU.max).then_inc(a_peak, 1)
            chunks(v, (0, peaks))
            v.wait_ge(a_peak, CHUNKS + RING)
            prev_reg = v.alloc_register("prev_window")
            lo_reg = v.alloc_register("window")
            further_reg = v.alloc_register("further")
            at_reg = v.alloc_register("at_window")

            def load_window(g):
                return (v.value_load(win_tab[0:1, 0, bass.ds(g, 1)], min_val=0, max_val=N - 1),
                        v.value_load(win_tab[0:1, 1, bass.ds(g, 1)], min_val=0, max_val=MAXW))

            def set_window(before, now):
                v.reg_mov(prev_reg, before)
                v.reg_mov(lo_reg, now[0])
                v.reg_mov(further_reg, now[1])

            def window():
                return (v.snap(lo_reg, min_val=0, max_val=N - 1), v.snap(further_reg, min_val=0, max_val=MAXW),
                        v.snap(prev_reg, min_val=0, max_val=N - 1))

            def scores(st, lo, u, wait_rows):
                st.link(v.tensor_tensor(by_tile(other[:, :]), over_window(dst_i[:, u, :]),
                                        over_tiles(iota[:, bass.ds(lo, WIN)]), ALU.not_equal))
                if wait_rows:
                    wait_rows()
                st.link(v.scalar_tensor_tensor(by_tile(other[:, :]), by_tile(other[:, :]), NEG,
                                               over_window(rows0(u)[:, :, D1]), ALU.mult, ALU.add))

            def largest(t):
                v.tensor_reduce(top[:, :], other[:, :].rearrange("p (j n) -> p n j", j=TILES), AX.X, ALU.max)\
                    .then_inc(t.top, 1)

            def shift(st, lo):
                st.step(v.tensor_tensor(by_tile(score[:, :]), by_tile(other[:, :]),
                                        over_tiles(adst[:, bass.ds(lo, WIN)]), ALU.add))

            def new_peak(st, t, n, lo, p_top_, p_topb_, between=None, ahead=None):
                here = bass.ds(lo, WIN)
                v.wait_ge(t.topt, n)
                st.step(v.tensor_reduce(top_col[:, :], p_top_, AX.X, ALU.max))
                column = st.n
                if between:
                    between()
                st.wait(column)
                v.tensor_scalar(top_diag[:, :], ident[0:WIN, 0:WIN], top_col[:, 0:1], None, ALU.mult)\
                    .then_inc(t.diag, 1)
                v.scalar_tensor_tensor(score[:, :], score[:, :], SLOPE, score[:, :], ALU.mult, ALU.max)
                v.wait_ge(t.topb, n)
                st.link(v.tensor_tensor(cand[:, :], p_topb_, adst[:, here], ALU.add))
                st.link(v.scalar_tensor_tensor(cand[:, :], cand[:, :], SLOPE, cand[:, :], ALU.mult, ALU.max))
                st.link(v.tensor_tensor(newp[:, :], cand[:, :], peak[:, here], ALU.max))
                st.step(v.tensor_tensor(drop[:, :], peak[0:D1, here], newp[0:D1, :], ALU.subtract))
                v.tensor_tensor(by_tile(score[:, :]), by_tile(score[:, :]), over_tiles(newp[:, :]), ALU.subtract)\
                    .then_inc(t.score, 1)
                got = ahead() if ahead else None
                st.wait()
                st.step(v.tensor_tensor(peak[:, here], cand[:, :], peak[:, here], ALU.max))
                return got

            def pad_last(e):
                v.memset(dst_i[:, 0, :], -1).then_inc(e.pad, 1)

            STEPS0 = 10
            STEPSX = 11

            def attend(g, it, u):
                lo, further, prev = window()
                if g is LAST:
                    pad_last(e0)
                st = Steps(v, e0.v, g * STEPS0, STEPS0)
                v.wait_ge(e0.dst[u], 16 * (it + 1))
                scores(st, lo, u, lambda: v.wait_ge(e0.rows[u], 16 * TILES * (it + 1)))
                largest(t0)
                before_here = bass.ds(prev, WIN)
                v.wait_ge(e0.acc, g + 1)
                shift(st, lo)
                st.step(v.tensor_tensor(acc[:, before_here], acc[:, before_here], fade[:, :], ALU.mult))
                faded = st.n

                def add_before():
                    st.wait(faded)
                    v.tensor_tensor(acc[:, before_here], acc[:, before_here], p_acc0, ALU.add).then_inc(e0.free, 1)
                after = new_peak(st, t0, g + 1, lo, p_top, p_topb, add_before,
                                 None if g is LAST else lambda: load_window(g + 1))
                st.done()
                with v.If(further > 0):
                    before = v.value_load(win_tab[0:1, 2, bass.ds(g, 1)], min_val=0, max_val=GROUPS * MAXW)
                    v.reg_mov(at_reg, lo)
                    with v.Fori(0, further) as k:
                        v.wait_ge(e0.acc, g + 2)
                        v.reg_add(at_reg, at_reg, WIN)
                        at = v.snap(at_reg, min_val=0, max_val=N - 1)
                        n = v.snap(before + k, min_val=0, max_val=GROUPS * MAXW)
                        sx = Steps(v, x0_v, n * STEPSX, STEPSX)
                        scores(sx, at, u, None)
                        largest(tx)
                        shift(sx, at)
                        new_peak(sx, tx, n + 1, at, px_top, px_topb)
                        v.wait_ge(x0_acc, n + 1)
                        sx.link(v.tensor_tensor(acc[:, bass.ds(at, WIN)], acc[:, bass.ds(at, WIN)], fade_x[:, :], ALU.mult))
                        sx.link(v.tensor_tensor(acc[:, bass.ds(at, WIN)], acc[:, bass.ds(at, WIN)], px_acc0, ALU.add))
                        sx.done()
                if g is not LAST:
                    set_window(lo, after)
                return lo

            set_window(0, load_window(0))
            prev = groups(v, attend)
            v.wait_ge(e0.acc, GROUPS + 1)
            v.tensor_tensor(acc[:, bass.ds(prev, WIN)], acc[:, bass.ds(prev, WIN)], fade[:, :], ALU.mult).then_inc(s_v, 1)
            v.wait_ge(s_v, 8)
            v.tensor_tensor(acc[:, bass.ds(prev, WIN)], acc[:, bass.ds(prev, WIN)], p_acc0, ALU.add).then_inc(e0.free, 1)

            def statistics(st, y, u, made):
                for b in range(CB):
                    last = v.bn_stats(bst[:, b, :], y[:, b, :])
                st.link(last)
                v.sem_inc(s_mark, 1)
                for b in range(CB):
                    last = v.bn_aggr(mv[:, u, 2 * b:2 * b + 2], bst[:, b, :])
                st.link(last)
                v.tensor_scalar(var[:, u, :], mv[:, u, :].rearrange("p (b k) -> p b k", k=2)[:, :, 1], EPS, None,
                                ALU.add).then_inc(made, 1)

            def normed(to, y, u):
                for b in range(CB):
                    last = v.tensor_scalar(to[:, b, :], y[:, b, :], mv[:, u, 2 * b:2 * b + 1], rstd[:, u, b:b + 1],
                                           ALU.subtract, ALU.mult)
                return last

            def inverted(c, u):
                v.wait_ge(m_t, c + 1)
                st = Steps(v, m_vd, c, 1)
                st.link(v.tensor_scalar(den[:, u, :], by_block(bank[u][:, :], D1)[:, :, D], 1e-16, None, ALU.add))
                v.reciprocal(rden[:, u, :], den[:, u, :]).then_inc(m_rden, 1)

            def added(c, u):
                st = Steps(v, m_v, c * 3, 3)
                v.wait_ge(m_th, c + 1)
                y = by_block(rowu[:, u, :])
                st.link(v.tensor_tensor(y, y, x1[:, bass.ds(c * CB, CB), :], ALU.add))
                statistics(st, y, u, m_var)
                st.done()

            def norm1(c, u):
                v.wait_ge(m_rstd, c + 1)
                normed(by_block(xs[:, u, :]), by_block(rowu[:, u, :]), u).then_inc(m_x1, 1)
            
            def sums(c, u):
                v.tensor_copy(colv[:, u, :], acc[:, columns(c)]).then_inc(m_col, 1)

            def keep_columns(c, u):
                v.wait_ge(m_colw, c + 1)
                v.tensor_copy(acc[0:D, columns(c)], colw[0:D, u, :]).then_inc(m_kc, 1)
            v.wait_ge(e0.free, GROUPS + SLOTS)
            chunks(v, (0, norm1), (4, sums), (1, added), (3, inverted), (0, keep_columns))
            v.wait_ge(m_kc, CHUNKS)

            def message(g, it, u):
                lo, further, prev = window()
                if g is LAST:
                    pad_last(e1)
                v.wait_ge(e1.dst[u], 16 * (it + 1))
                v.tensor_tensor(by_tile(onehot[:, u, :]), over_window(dst_i[:, u, :]),
                                over_tiles(iota[:, bass.ds(lo, WIN)]), ALU.is_equal).then_inc(e1_hot, 1)
                v.wait_ge(e1.rows[u], 16 * TILES * (it + 1))
                v.wait_ge(e1.attr[u], 16 * (it + 1))
                v.tensor_tensor(rows[:, u, 0:TILES * D], rows[:, u, 0:TILES * D], attr[:, u, :], ALU.mult)\
                    .then_inc(e1_msg, 1)
                v.wait_ge(e1.free, g + SLOTS - 1)
                v.wait_ge(e1.acc, g + 1)
                here = bass.ds(prev, WIN)
                v.tensor_tensor(acc[0:D, here], acc[0:D, here], p_acc1[(u - 1) % SLOTS], ALU.add).then_inc(e1.free, 1)
                after = None if g is LAST else load_window(g + 1)
                with v.If(further > 0):
                    before = v.value_load(win_tab[0:1, 2, bass.ds(g, 1)], min_val=0, max_val=GROUPS * MAXW)
                    v.reg_mov(at_reg, lo)
                    with v.Fori(0, further) as k:
                        v.reg_add(at_reg, at_reg, WIN)
                        at = v.snap(at_reg, min_val=0, max_val=N - 1)
                        v.tensor_tensor(by_tile(onehot_x[:, :]), over_window(dst_i[:, u, :]),
                                        over_tiles(iota[:, bass.ds(at, WIN)]), ALU.is_equal).then_inc(x1_hot, 1)
                        v.wait_ge(x1_acc, before + k + 1)
                        v.wait_ge(e1.free, g + SLOTS)
                        v.tensor_tensor(acc[0:D, bass.ds(at, WIN)], acc[0:D, bass.ds(at, WIN)], px_acc1, ALU.add)\
                            .then_inc(x1_v, 1)
                        v.wait_ge(x1_v, before + k + 1)
                if g is not LAST:
                    set_window(lo, after)
                return lo

            set_window(0, load_window(0))
            v.wait_ge(m_g, CHUNKS)
            prev = groups(v, message)
            v.wait_ge(e1.acc, GROUPS + 1)
            v.wait_ge(e1.free, GROUPS + SLOTS - 1)
            v.tensor_tensor(acc[0:D, bass.ds(prev, WIN)], acc[0:D, bass.ds(prev, WIN)], p_acc1[0], ALU.add)\
                .then_inc(e1.free, 1)
            v.wait_ge(e1.free, GROUPS + SLOTS)

            def plus_input(c, u):
                v.wait_ge(f_g2, c + 1)
                v.tensor_tensor(colv[0:D, u, :], colv[0:D, u, :], acc[0:D, columns(c)], ALU.add).then_inc(f_s, 1)

            def residual(c, u):
                st = Steps(v, f_v, c * 3, 3)
                v.wait_ge(f_t, c + 1)
                y = by_block(rowu[:, u, :])
                st.link(v.tensor_tensor(y, by_block(bank[3 + u][:, :]), x1[:, bass.ds(c * CB, CB), :], ALU.add))
                statistics(st, y, u, f_var)
                st.done()

            def norm2(c, u):
                v.wait_ge(f_rstd, c + 1)
                v.wait_ge(f_free, c + 1)
                normed(by_block(rowt[:, u, :]), by_block(rowu[:, u, :]), u).then_inc(f_o, 1)
            chunks(v, (0, norm2), (1, residual), (2, plus_input))


_INS = ['x', 'src', 'dst', 'edge_attr_96', 'L0_gnn_W', 'L0_gnn_att_src', 'L0_gnn_att_dst', 'L0_gnn_bias',
        'L1_gnn_W_pre', 'L1_gnn_b_pre', 'L1_gnn_W1', 'L1_gnn_b1', 'L1_gnn_W2', 'L1_gnn_b2']


def kernel(**inputs):
    import numpy as _np
    import concourse.bacc as _bacc
    from concourse import mybir as _mybir
    from concourse.bass_utils import run_bass_kernel_spmd as _run

    nc = _bacc.Bacc("TRN2", target_bir_lowering=False, num_devices=1)
    arrays, args = {}, []
    for name in _INS:
        a = _np.ascontiguousarray(inputs[name])
        arrays[f"in_{name}_dram"] = a
        args.append(nc.dram_tensor(f"in_{name}_dram", a.shape, _mybir.dt.from_np(a.dtype), kind="ExternalInput").ap())
    shape = inputs['x'].shape
    args.append(nc.dram_tensor("out_0_dram", shape, _mybir.dt.float32, kind="ExternalOutput").ap())
    gnn(nc, *args)
    r = _run(nc, [arrays], core_ids=[0])
    return r.results[0]["out_0_dram"]
```

```python
from contextlib import ExitStack

import concourse.bass as bass
from concourse import mybir

FP32 = mybir.dt.float32
INT32 = mybir.dt.int32
ALU = mybir.AluOpType
ACT = mybir.ActivationFunctionType
AX = mybir.AxisListType

P = 128
TILES = 8
SLOTS = 5
RING = 3
WIN = 72
FAR = 2.0 ** 50
NEG = -1e30
SLOPE = 0.2
EPS = 1e-5
CB = 4


def gnn(nc, x, src, dst, edge_attr, w0, att_src, att_dst, bias0, w_pre, b_pre, w1, b1, w2, b2, out):
    N, D = x.shape
    E = src.shape[0]
    GE = P * TILES
    GROUPS = -(-E // GE)
    ROUNDS = (GROUPS - 1) // SLOTS
    LAST = GROUPS - 1
    LAST_E = E - LAST * GE
    LAST_T = next(t for t in range(1, TILES + 1) if LAST_E % t == 0 and LAST_E // t <= P)
    assert LAST == ROUNDS * SLOTS
    D1 = D + 1
    D2 = D + 2
    CN = CB * P
    CHUNKS = -(-N // CN)
    LAST_N = N - (CHUNKS - 1) * CN
    assert LAST_N <= P and CHUNKS % RING == 1
    FULL = N // P
    NP = CHUNKS * CN
    assert NP >= N + WIN
    TG = GROUPS // 2
    assert GROUPS == 2 * TG and TG <= P
    MB = 3
    MN = MB * P
    MCHUNKS = -(-(FULL + 1 - CB) // MB)
    REST_B = FULL + 1 - MCHUNKS * MB
    assert 1 <= REST_B <= CB
    STORED = 16 * (MCHUNKS + 2 + (REST_B > 1))
    DUE = 16
    assert MCHUNKS < DUE
    MAXW = -(-(N - 1) // WIN)
    BITS = N.bit_length()

    ctx = ExitStack()
    with ctx:
        def sb(name, shape, dt=FP32):
            return ctx.enter_context(nc.sbuf_tensor(name, shape, dt))

        def sem(name):
            return ctx.enter_context(nc.semaphore(name))

        def sems(name, n):
            return [sem(f"{name}{i}") for i in range(n)]

        table0 = nc.dram_tensor("table0", (N, D2), FP32, kind="Internal").ap()
        table1 = nc.dram_tensor("table1", (N, D), FP32, kind="Internal").ap()

        iota = sb("iota", [P, NP], mybir.dt.int16)
        adst = sb("adst", [P, NP])
        peak = sb("peak", [P, NP])
        acc = sb("acc", [D1, NP])
        x1 = sb("x1", [P, NP // P, D2])

        src_i = sb("src_i", [P, SLOTS, TILES], INT32)
        dst_i = sb("dst_i", [P, SLOTS, TILES], INT32)
        rows = sb("rows", [P, SLOTS, TILES * D2])
        attr = sb("attr", [P, SLOTS, TILES * D])
        onehot = sb("onehot", [P, SLOTS, TILES * WIN])

        other = sb("other", [P, TILES * WIN])
        score = sb("score", [P, TILES * WIN])
        top = sb("top", [P, WIN])
        top_col = sb("top_col", [WIN, 1])
        top_diag = sb("top_diag", [WIN, WIN])
        cand = sb("cand", [P, WIN])
        newp = sb("newp", [P, WIN])
        drop = sb("drop", [D1, WIN])
        fade = sb("fade", [D1, SLOTS, WIN])
        fade_x = sb("fade_x", [D1, WIN])
        onehot_x = sb("onehot_x", [P, TILES * WIN])
        no_node = sb("no_node", [P, TILES], INT32)
        far_dst = sb("far_dst", [P, SLOTS, TILES])

        ident = sb("ident", [P, P])
        ones = sb("ones", [P, P])
        zeros = sb("zeros", [P, P])
        w0x = sb("w0x", [D1, D1])
        w0t = sb("w0t", [D, D])
        att = sb("att", [D, 2])
        att_wide = sb("att_wide", [D, P])
        w0att = sb("w0att", [D, 2])
        w0src = sb("w0src", [P, D])
        w0dst = sb("w0dst", [D, P])
        w0both = sb("w0both", [D, P])
        w_prex = sb("w_prex", [D1, D])
        w1s = sb("w1s", [D, D])
        w2s = sb("w2s", [D, D])
        b1s = sb("b1s", [D, 1])
        b2s = sb("b2s", [D, 1])

        xs = sb("xs", [P, RING, CB * D])
        zcol = sb("zcol", [P, RING, CN])
        rowu = sb("rowu", [P, RING, CB * D])
        colw = sb("colw", [D1, 1, CN])
        colv = sb("colv", [D1, 1, CN])
        rowt = sb("rowt", [P, 1, CB * D])
        den = sb("den", [P, 1, CB])
        rden = sb("rden", [P, 1, CB])
        bst = sb("bst", [P, CB, 6])
        mv = sb("mv", [P, 1, 2 * CB])
        var = sb("var", [P, 2, CB])
        rstd = sb("rstd", [P, 1, CB])
        newton = sb("newton", [P, CB])

        dsts = attr[0:TG, :, :].rearrange("p s n -> p (s n)")[:, 0:2 * GE].bitcast(INT32)\
            .rearrange("p (k e) -> p k e", k=2)
        low = sb("low", [TG, 2])
        high = sb("high", [TG, 2])
        steps_i = sb("steps_i", [TG, MAXW], INT32)
        more = sb("more", [TG, 2, MAXW])
        extra = sb("extra", [TG, 2])
        line = sb("line", [1, 2, GROUPS])
        upto = sb("upto", [1, GROUPS])
        run = sb("run", [1, GROUPS])
        win_tab = sb("win_tab", [1, 3, GROUPS + 1], INT32)
        group_no = sb("group_no", [TG, 2], INT32)
        chunk_end = sb("chunk_end", [TG, MCHUNKS], INT32)
        begun = sb("begun", [TG, MCHUNKS, 2])
        begun_col = sb("begun_col", [2 * MCHUNKS, 1])
        since = sb("since", [1, MCHUNKS])
        ready = onehot[0:1, :, :].rearrange("p s n -> p (s n)")[:, 0:ROUNDS * MCHUNKS]\
            .rearrange("p (r c) -> p r c", c=MCHUNKS)
        ready_n = sb("ready_n", [1, ROUNDS + 2])
        due_tab = sb("due_tab", [1, ROUNDS + 1], INT32)

        bank = [ctx.enter_context(nc.psum_tensor(f"bank{i}", [P, 512], FP32)) for i in range(8)]

        parts = [(0, 2), (2, 4), (4, 8), (8, CHUNKS - 1)]
        s_x = sems("s_x", len(parts) + 1)
        s_w0 = sem("s_w0")
        s_w = sem("s_w")
        s_dsts = sem("s_dsts")
        s_const = sem("s_const")
        s_fill = sem("s_fill")
        s_prep = sem("s_prep")
        s_prepc = sem("s_prepc")
        s_line = sem("s_line")
        s_begun = sem("s_begun")
        s_since = sem("s_since")
        s_tab0 = sem("s_tab0")
        s_tab = sem("s_tab")
        s_mark = sem("s_mark")
        s_v = sem("s_v")

        a_in = sem("a_in")
        a_row = sem("a_row")
        a_st = sem("a_st")
        a_v = sem("a_v")
        a_x = sem("a_x")
        a_t = sem("a_t")
        a_tc = sem("a_tc")
        a_col = sem("a_col")
        a_colc = sem("a_colc")
        a_peak = sem("a_peak")
        m_col = sem("m_col")
        m_t = sem("m_t")
        m_rden = sem("m_rden")
        m_th = sem("m_th")
        m_var = sem("m_var")
        m_dev = sem("m_dev")
        m_x1 = sem("m_x1")
        m_x1t = sem("m_x1t")
        m_colw = sem("m_colw")
        m_kept = sem("m_kept")
        m_h = sem("m_h")
        m_g = sem("m_g")
        m_st = sem("m_st")
        m_v = sem("m_v")
        f_go = sem("f_go")
        f_y1 = sem("f_y1")
        f_g1 = sem("f_g1")
        f_y2 = sem("f_y2")
        f_g2 = sem("f_g2")
        f_s = sem("f_s")
        f_t = sem("f_t")
        f_var = sem("f_var")
        f_dev = sem("f_dev")
        f_o = sem("f_o")
        f_st = sem("f_st")
        f_v = sem("f_v")

        class Edge:
            def __init__(self, n):
                self.src = sems(f"e{n}_src", SLOTS)
                self.dst = sems(f"e{n}_dst", SLOTS)
                self.attr = sems(f"e{n}_attr", SLOTS)
                self.rows = sems(f"e{n}_rows", SLOTS)
                self.go = sem(f"e{n}_go")
                self.free = sem(f"e{n}_free")
                self.pad = sem(f"e{n}_pad")
                self.acc = sem(f"e{n}_acc")
                self.v = sem(f"e{n}_v")

        class Top:
            def __init__(self, n):
                self.top = sem(f"{n}_top")
                self.topt = sem(f"{n}_topt")
                self.away = sem(f"{n}_away")
                self.diag = sem(f"{n}_diag")
                self.topb = sem(f"{n}_topb")
                self.score = sem(f"{n}_score")
                self.w = sem(f"{n}_w")

        e0, e1 = Edge(0), Edge(1)
        t0, tx = Top("t0"), Top("tx")
        x0_acc, x1_acc = sem("x0_acc"), sem("x1_acc")
        x0_v, x1_v = sem("x0_v"), sem("x1_v")
        e0_far = sem("e0_far")
        e1_hot, e1_msg, x1_hot = sem("e1_hot"), sem("e1_msg"), sem("x1_hot")

        p_top, px_top = bank[0][0:WIN, 0:P], bank[3][0:WIN, 0:P]
        p_topb, px_topb = bank[1][:, 0:WIN], bank[4][:, 0:WIN]
        p_acc0, px_acc0 = bank[2][0:D1, 0:WIN], bank[5][0:D1, 0:WIN]
        p_node, p_node2 = bank[6], bank[7]
        p_line = bank[7][0:1, 0:2 * GROUPS]
        p_begun = bank[7][0:2 * MCHUNKS, 2 * GROUPS:2 * GROUPS + TG]
        p_since = bank[7][0:1, 0:2 * MCHUNKS]
        p_acc1, px_acc1 = [bank[i][0:D, 0:WIN] for i in range(SLOTS)], bank[5][0:D, 0:WIN]
        assert SLOTS <= 5

        def by_tile(t):
            return t.rearrange("p (j n) -> p j n", j=TILES)

        def rows0(u):
            return rows[:, u, :].rearrange("p (j d) -> p j d", j=TILES)

        def rows1(u):
            return rows[:, u, 0:TILES * D].rearrange("p (j d) -> p j d", j=TILES)

        def over_tiles(t):
            return t[:, None, :].broadcast_to([P, TILES, WIN])

        def over_window(t):
            return t[:, :, None].broadcast_to([P, TILES, WIN])

        def by_block(t, w=D):
            return t[:, 0:CB * w].rearrange("p (b d) -> p b d", d=w)

        def columns(c):
            return bass.ds(c * CN, CN)

        def groups(eng, body, after_round=None):
            with eng.Fori(0, ROUNDS) as it:
                for u in range(SLOTS):
                    body(it * SLOTS + u, it, u)
                if after_round:
                    after_round(it)
            return body(LAST, ROUNDS, 0)

        due_regs = {}

        def due(eng, k, body):
            packed = eng.value_load(due_tab[0:1, bass.ds(k, 1)], min_val=0, max_val=(MCHUNKS + 1) * DUE)
            with eng.If((packed & (DUE - 1)) > 0):
                if eng not in due_regs:
                    due_regs[eng] = eng.alloc_register("due"), eng.alloc_register("chunk")
                n_reg, chunk_reg = due_regs[eng]
                eng.reg_alu(n_reg, packed, DUE - 1, ALU.bitwise_and)
                eng.reg_alu(chunk_reg, packed, DUE.bit_length() - 1, ALU.logical_shift_right)
                with eng.Fori(0, eng.snap(n_reg, min_val=0, max_val=MCHUNKS)):
                    body(eng.snap(chunk_reg, min_val=0, max_val=MCHUNKS - 1))
                    eng.reg_add(chunk_reg, chunk_reg, 1)

        def rest(eng, body):
            due(eng, ROUNDS, body)
            body(MCHUNKS, REST_B)

        def nodes(c, blocks):
            return bass.ds(c * MN, blocks * P)

        def chunks(eng, *stages, enter=None):
            most = max(lead for lead, _ in stages)
            rounds = (CHUNKS - most) // RING

            def peeled(t):
                for lead, body in stages:
                    c = t + lead
                    if 0 <= c < CHUNKS:
                        body(c, c % RING, c // RING)
            for t in range(-most, 0):
                peeled(t)
            if enter:
                enter()
            with eng.Fori(0, rounds) as it:
                for u in range(RING):
                    for lead, body in stages:
                        body(it * RING + (u + lead), (u + lead) % RING, it + (u + lead) // RING)
            for t in range(rounds * RING, CHUNKS):
                peeled(t)

        def gathered(g, it):
            return 16 * (TILES * it + (LAST_T if g is LAST else TILES))

        class Steps:
            def __init__(self, eng, s, base, most):
                self.eng, self.s, self.base, self.n, self.most = eng, s, base, 0, most

            def step(self, ins):
                self.n += 1
                assert self.n <= self.most
                ins.then_inc(self.s, 1)

            def wait(self, n=None):
                self.eng.wait_ge(self.s, self.base + (n or self.n))

            def link(self, ins):
                self.step(ins)
                self.wait()

            def done(self):
                assert self.n == self.most

        block = ctx.enter_context(nc.Block())

        @block.sync
        def _(sp):
            sp.dma_start(w0x[0:D, 0:D], w0).then_inc(s_w0, 16)
            sp.dma_start(att[:, 0:1], att_src.rearrange("(d a) -> d a", a=1)).then_inc(s_w0, 16)
            sp.dma_start(att[:, 1:2], att_dst.rearrange("(d a) -> d a", a=1)).then_inc(s_w0, 16)
            for i, (a, b) in enumerate(parts):
                sp.dma_start(x1[:, a * CB:b * CB, 0:D], x[a * CN:b * CN, :].rearrange("(b p) d -> p b d", p=P))\
                    .then_inc(s_x[i], 16)
            sp.wait_ge(s_fill, 1)
            sp.dma_start(x1[0:LAST_N, (CHUNKS - 1) * CB, 0:D], x[(CHUNKS - 1) * CN:N, :]).then_inc(s_x[-1], 16)
            for i, (a, b) in enumerate(parts):
                sp.wait_ge(s_x[i], 16)
                sp.sem_inc(a_in, b - a)
            sp.wait_ge(s_x[-1], 16)
            sp.sem_inc(a_in, 1)

            def store_table():
                with sp.Fori(0, CHUNKS - 1) as c:
                    sp.wait_ge(a_row, c + 1)
                    sp.dma_start(table0[bass.ds(c * CN, CN), :].rearrange("(b p) d -> p b d", p=P),
                                 x1[:, bass.ds(c * CB, CB), :]).then_inc(a_st, 16)
                sp.wait_ge(a_row, CHUNKS)
                sp.dma_start(table0[(CHUNKS - 1) * CN:N, :], x1[0:LAST_N, (CHUNKS - 1) * CB, :]).then_inc(a_st, 16)

            def load_edges(e, attrs):
                def body(g, it, u):
                    n, t = (LAST_E, LAST_T) if g is LAST else (GE, TILES)
                    m = n // t
                    sp.wait_ge(e.free, g + 1)
                    sp.dma_start(src_i[0:m, u, 0:t], src[bass.ds(g * GE, n)].rearrange("(p j) -> p j", j=t))\
                        .then_inc(e.src[u], 16)
                    if g is LAST:
                        sp.dma_start(dst_i[:, u, :], no_node[:, :]).then_inc(e.pad, 16)
                        sp.wait_ge(e.pad, 16)
                    sp.dma_start(dst_i[0:m, u, 0:t], dst[bass.ds(g * GE, n)].rearrange("(p j) -> p j", j=t))\
                        .then_inc(e.dst[u], 16)
                    if attrs:
                        sp.dma_start(attr[0:m, u, 0:t * D],
                                     edge_attr[bass.ds(g * GE, n), :].rearrange("(p j) d -> p (j d)", j=t))\
                            .then_inc(e.attr[u], 16)
                return body

            store_table()
            groups(sp, load_edges(e0, False))
            sp.wait_ge(e0.free, GROUPS + SLOTS)
            groups(sp, load_edges(e1, True))

        @block.gpsimd
        def _(pool):
            pool.memset(ident[:, :], 0.0).then_inc(s_const, 1)
            pool.wait_ge(s_const, 1)
            pool.affine_select(out=ident[:, :], in_=ident[:, :], compare_op=ALU.not_equal, fill=1.0,
                               base=0, pattern=[[-1, P]], channel_multiplier=1).then_inc(s_const, 1)
            pool.iota(group_no[:, :], pattern=[[TG, 2]], base=1, channel_multiplier=1)
            pool.iota(chunk_end[:, :], pattern=[[MN, MCHUNKS]], base=MN, channel_multiplier=0)
            pool.iota(steps_i[:, :], pattern=[[WIN, MAXW]], base=WIN, channel_multiplier=0).then_inc(s_const, 1)
            pool.iota(iota[:, :], pattern=[[1, NP]], base=0, channel_multiplier=0).then_inc(s_const, 1)
            pool.wait_ge(s_const, 4)
            pool.memset(acc[D:D1, :], 1.0).then_inc(s_const, 1)

            def gather(e, table, width):
                def body(g, it, u):
                    pool.wait_ge(e.src[u], 16 * (it + 1))
                    pool.sem_inc(e.go, 1)
                    for j in range(LAST_T if g is LAST else TILES):
                        pool.indirect_dma_start(rows[:, u, j * width:(j + 1) * width], None, table,
                                                bass.IndirectOffsetOnAxis(ap=src_i[:, u, j:j + 1], axis=0))\
                            .then_inc(e.rows[u], 16)
                return body

            pool.wait_ge(a_st, 16 * CHUNKS)
            groups(pool, gather(e0, table0, D2))
            pool.wait_ge(m_st, STORED)
            groups(pool, gather(e1, table1, D))

        @block.scalar
        def _(act):
            act.dma_start(dsts[:, 0, :], dst[0:TG * GE].rearrange("(p e) -> p e", e=GE)).then_inc(s_dsts, 16)
            act.dma_start(dsts[0:TG - 1, 1, :], dst[TG * GE:LAST * GE].rearrange("(p e) -> p e", e=GE))\
                .then_inc(s_dsts, 16)
            tail = E - LAST * GE
            rep = 64
            assert (GE - tail) % rep == 0 and tail >= rep
            act.dma_start(dsts[TG - 1:TG, 1, 0:tail], dst[LAST * GE:E].rearrange("(p e) -> p e", p=1))\
                .then_inc(s_dsts, 16)
            act.dma_start(dsts[TG - 1:TG, 1, tail:GE].rearrange("p (a b) -> p a b", b=rep),
                          dst[E - rep:E].rearrange("(p a b) -> p a b", p=1, a=1)
                          .broadcast_to([1, (GE - tail) // rep, rep])).then_inc(s_dsts, 16)
            act.dma_start(w_prex[0:D, :], w_pre).then_inc(s_w, 16)
            act.dma_start(w_prex[D:D1, :], b_pre.rearrange("(a d) -> a d", a=1)).then_inc(s_w, 16)
            act.dma_start(w1s[:, :], w1).then_inc(s_w, 16)
            act.dma_start(w2s[:, :], w2).then_inc(s_w, 16)
            act.dma_start(b1s[:, :], b1.rearrange("(d a) -> d a", a=1)).then_inc(s_w, 16)
            act.dma_start(b2s[:, :], b2.rearrange("(d a) -> d a", a=1)).then_inc(s_w, 16)
            act.dma_start(w0x[D:D1, 0:D], bias0.rearrange("(a d) -> a d", a=1)).then_inc(s_w, 16)

            def turned(c, u, r):
                act.wait_ge(a_t, c + 1)
                act.activation(acc[0:D, columns(c)], bank[6][0:D, :], ACT.Copy).then_inc(a_tc, 1)

            def columns0(c, u, r):
                act.wait_ge(a_col, c + 1)
                act.activation(adst[:, columns(c)], bank[u][:, :], ACT.Copy)
                act.activation(zcol[:, u, :], bank[3 + u][:, :], ACT.Copy, scale=SLOPE).then_inc(a_colc, 1)
            act.sem_inc(a_tc, 1)
            chunks(act, (1, turned), (0, columns0))

            def away(g, it, u):
                first = act.value_load(win_tab[0:1, 0, bass.ds(g, 1)], min_val=0, max_val=(MAXW + 1) << BITS)
                act.reg_alu(act_lo, first, (1 << BITS) - 1, ALU.bitwise_and)
                lo = act.snap(act_lo, min_val=0, max_val=N - 1)
                act.wait_ge(e0.dst[u], 16 * (it + 1))
                act.activation(far_dst[:, u, :], dst_i[:, u, :], ACT.Copy, scale=-FAR).then_inc(e0_far, 1)
                act.wait_ge(e0_far, g + 1)
                for j in range(TILES):
                    last = act.activation(by_tile(onehot[:, u, :])[:, j, :], iota[:, bass.ds(lo, WIN)], ACT.Square,
                                          scale=FAR, bias=far_dst[:, u, j:j + 1])
                last.then_inc(t0.away, 1)
            act_lo = act.alloc_register("window")

            def weights(g, it, u):
                if g is not LAST and u > 0:
                    away(g + 1, it + (u + 1) // SLOTS, (u + 1) % SLOTS)
                act.wait_ge(t0.score, g + 1)
                act.activation(fade[:, u, :], drop[:, :], ACT.Exp)
                act.activation(onehot[:, u, :], score[:, :], ACT.Exp).then_inc(t0.w, 1)
                further = act.value_load(win_tab[0:1, 1, bass.ds(g, 1)], min_val=0, max_val=MAXW)
                with act.If(further > 0):
                    before = act.value_load(win_tab[0:1, 2, bass.ds(g, 1)], min_val=0, max_val=GROUPS * MAXW)
                    with act.Fori(0, further) as k:
                        act.wait_ge(tx.score, before + k + 1)
                        act.activation(fade_x[:, :], drop[:, :], ACT.Exp)
                        act.activation(onehot_x[:, :], score[:, :], ACT.Exp).then_inc(tx.w, 1)
                if g is not LAST and u == SLOTS - 1:
                    with act.If(it < ROUNDS - 1):
                        away(g + 2, it + 1, 1)
            act.wait_ge(s_tab, 2)
            def middle(c, blocks=MB):
                act.wait_ge(m_rden, c + 1)
                for b in range(blocks):
                    last = act.activation(rowu[:, 0, b * D:(b + 1) * D], p_node[:, b * D1:b * D1 + D], ACT.Tanh,
                                          scale=rden[:, 0, b:b + 1])
                last.then_inc(m_th, 1)
                act.wait_ge(m_var, c + 1)
                act.activation(var[:, 1, 0:blocks], var[:, 0, 0:blocks], ACT.Sqrt).then_inc(m_dev, 1)
                act.wait_ge(m_x1t, c + 1)
                act.activation(colw[0:D, 0, 0:blocks * P], p_node2[0:D, 0:blocks * P], ACT.Copy)
                act.activation(acc[0:D, nodes(c, blocks)], p_node2[0:D, 0:blocks * P], ACT.Copy).then_inc(m_colw, 1)
                act.wait_ge(m_h, c + 1)
                act.wait_ge(m_st, 16 * (c + 1))
                act.activation(rowt[:, 0, 0:blocks * D], p_node2[:, 0:blocks * D], ACT.Gelu).then_inc(m_g, 1)
                act.wait_ge(m_g, c + 1)
                store(table1, c, blocks, m_st)
                act.activation(x1[:, bass.ds(c * MB, blocks), 0:D], by_block(xs[:, 0, :])[:, 0:blocks, :], ACT.Copy)\
                    .then_inc(m_kept, 1)

            def store(dram, c, blocks, stored):
                if c is not MCHUNKS:
                    act.dma_start(dram[bass.ds(c * MN, MN), :].rearrange("(b p) d -> p b d", p=P),
                                  by_block(rowt[:, 0, :])[:, 0:MB, :]).then_inc(stored, 16)
                    return
                full = blocks - 1
                if full:
                    act.dma_start(dram[c * MN:FULL * P, :].rearrange("(b p) d -> p b d", p=P),
                                  by_block(rowt[:, 0, :])[:, 0:full, :]).then_inc(stored, 16)
                act.dma_start(dram[FULL * P:N, :], by_block(rowt[:, 0, :])[0:N - FULL * P, full, :]).then_inc(stored, 16)

            act.sem_inc(t0.w, 1)
            act.sem_inc(m_st, 16)
            act.sem_inc(f_st, 16)
            away(0, 0, 0)
            away(1, 0, 1)
            groups(act, weights, lambda it: due(act, it, middle))
            rest(act, middle)

            def final(c, blocks=MB):
                act.wait_ge(f_y1, c + 1)
                act.activation(colw[0:D, 0, 0:blocks * P], p_node[0:D, 0:blocks * P], ACT.Gelu, bias=b1s[:, 0:1])\
                    .then_inc(f_g1, 1)
                act.wait_ge(f_y2, c + 1)
                act.activation(colv[0:D, 0, 0:blocks * P], p_node2[0:D, 0:blocks * P], ACT.Gelu, bias=b2s[:, 0:1])\
                    .then_inc(f_g2, 1)
                act.wait_ge(f_st, 16 * (c + 1))
                act.wait_ge(f_var, c + 1)
                act.activation(var[:, 1, 0:blocks], var[:, 0, 0:blocks], ACT.Sqrt).then_inc(f_dev, 1)
                act.wait_ge(f_o, c + 1)
                store(out, c, blocks, f_st)
            with act.Fori(0, ROUNDS) as it:
                due(act, it, final)
            rest(act, final)
            act.wait_ge(f_st, STORED)

        @block.tensor
        def _(pe):
            pe.wait_ge(s_w0, 16 * 3)
            pe.wait_ge(s_const, 2)
            pe.wait_ge(s_fill, 2)
            pe.transpose(bank[7][0:D, 0:D], w0x[0:D, 0:D], ident[0:D, 0:D]).then_inc(s_prep, 1)
            pe.wait_ge(s_prepc, 1)
            pe.matmul(bank[7][0:D, 128:130], w0t[:, :], att[:, :], start=True, stop=True).then_inc(s_prep, 1)
            pe.wait_ge(s_prepc, 2)
            pe.matmul(bank[7][:, 256:256 + D], att_wide[:, :], w0t[:, :], start=True, stop=True).then_inc(s_prep, 1)
            pe.wait_ge(s_prepc, 3)

            def turn(c, u, r):
                pe.wait_ge(a_x, c + 1)
                pe.wait_ge(a_tc, c + 1)
                for b in range(CB):
                    last = pe.transpose(bank[6][0:D, b * P:(b + 1) * P], xs[:, u, b * D:(b + 1) * D], ident[:, :])
                last.then_inc(a_t, 1)

            def by_column(c, u, r):
                xt = acc[0:D, columns(c)]
                pe.wait_ge(a_tc, c + 2)
                pe.wait_ge(a_peak, c + 1)
                pe.matmul(bank[u][:, :], w0dst[:, :], xt, start=True, stop=True)
                pe.matmul(bank[3 + u][:, :], w0both[:, :], xt, start=True, stop=True).then_inc(a_col, 1)
            chunks(pe, (1, turn), (0, by_column))

            pe.wait_ge(s_tab0, 1)
            for k in range(2):
                pe.matmul(p_line[:, k * TG:(k + 1) * TG], low[:, k:k + 1], ident[0:TG, 0:TG], start=True, stop=True)
                pe.matmul(p_line[:, GROUPS + k * TG:GROUPS + (k + 1) * TG], extra[:, k:k + 1],
                          ident[0:TG, 0:TG], start=True, stop=True)
            pe.transpose(p_begun, begun[:, :, :].rearrange("p c k -> p (c k)"), ident[0:TG, 0:TG])\
                .then_inc(s_line, 1)
            pe.wait_ge(s_begun, 1)
            pe.matmul(p_since, begun_col[:, :], ident[0:2 * MCHUNKS, 0:2 * MCHUNKS], start=True, stop=True)\
                .then_inc(s_since, 1)

            pe.wait_ge(a_peak, CHUNKS + RING)
            pe.matmul(p_acc0, zeros[:, 0:D1], zeros[:, 0:WIN], start=True, stop=True).then_inc(e0.acc, 1)
            pe.wait_ge(s_tab, 2)

            def spread_top(t, top_t, topb, n):
                pe.wait_ge(t.top, n)
                pe.transpose(top_t, top[:, :], ident[:, :]).then_inc(t.topt, 1)
                pe.wait_ge(t.diag, n)
                pe.matmul(topb, ones[0:WIN, :], top_diag[:, :], start=True, stop=True).then_inc(t.topb, 1)

            def window_sum(total, weights, u, tiles):
                for j in tiles:
                    last = pe.matmul(total, rows0(u)[:, j, 0:D1], by_tile(weights)[:, j, :],
                                     start=j == 0, stop=j == TILES - 1)
                return last

            def attend(g, it, u):
                further = pe.value_load(win_tab[0:1, 1, bass.ds(g, 1)], min_val=0, max_val=MAXW)
                with pe.If(further > 0):
                    before = pe.value_load(win_tab[0:1, 2, bass.ds(g, 1)], min_val=0, max_val=GROUPS * MAXW)
                    with pe.Fori(0, further) as k:
                        spread_top(tx, px_top, px_topb, before + k + 1)
                        pe.wait_ge(tx.w, before + k + 1)
                        window_sum(px_acc0, onehot_x[:, :], u, range(TILES)).then_inc(x0_acc, 1)
                pe.wait_ge(t0.w, g + 2)
                pe.wait_ge(e0.free, g + SLOTS)
                window_sum(p_acc0, onehot[:, u, :], u, range(TILES // 2))
                if g is not LAST and u == SLOTS - 1:
                    due(pe, it, middle)
                if g is not LAST:
                    spread_top(t0, p_top, p_topb, g + 2)
                window_sum(p_acc0, onehot[:, u, :], u, range(TILES // 2, TILES)).then_inc(e0.acc, 1)

            def middle(c, blocks=MB):
                pe.wait_ge(m_col, c + 1)
                for b in range(blocks):
                    last = pe.matmul(p_node[:, b * D1:(b + 1) * D1], colv[:, 0, b * P:(b + 1) * P], w0x[:, :],
                                     start=True, stop=True)
                last.then_inc(m_t, 1)
                pe.wait_ge(m_x1, c + 1)
                for b in range(blocks):
                    last = pe.transpose(p_node2[0:D, b * P:(b + 1) * P], xs[:, 0, b * D:(b + 1) * D], ident[:, :])
                last.then_inc(m_x1t, 1)
                pe.wait_ge(m_colw, c + 1)
                for b in range(blocks):
                    last = pe.matmul(p_node2[:, b * D:(b + 1) * D], colw[:, 0, b * P:(b + 1) * P], w_prex[:, :],
                                     start=True, stop=True)
                last.then_inc(m_h, 1)
            pe.wait_ge(s_w, 16 * 7)
            spread_top(t0, p_top, p_topb, 1)
            groups(pe, attend)
            rest(pe, middle)

            pe.matmul(p_acc1[SLOTS - 1], zeros[:, 0:D], zeros[:, 0:WIN], start=True, stop=True).then_inc(e1.acc, 1)

            def window1(total, hot, u, counted):
                for j in range(TILES):
                    last = pe.matmul(total, rows1(u)[:, j, :], by_tile(hot)[:, j, :],
                                     start=j == 0, stop=j == TILES - 1)
                last.then_inc(counted, 1)

            def gather_sum(g, it, u):
                pe.wait_ge(e1_hot, g + 1)
                pe.wait_ge(e1_msg, g + 1)
                window1(p_acc1[u], onehot[:, u, :], u, e1.acc)
                further = pe.value_load(win_tab[0:1, 1, bass.ds(g, 1)], min_val=0, max_val=MAXW)
                with pe.If(further > 0):
                    before = pe.value_load(win_tab[0:1, 2, bass.ds(g, 1)], min_val=0, max_val=GROUPS * MAXW)
                    with pe.Fori(0, further) as k:
                        pe.wait_ge(x1_hot, before + k + 1)
                        window1(px_acc1, onehot_x[:, :], u, x1_acc)

            def final(c, blocks=MB):
                pe.wait_ge(f_go, c + 1)
                pe.matmul(p_node[0:D, 0:blocks * P], w1s[:, :], acc[0:D, nodes(c, blocks)], start=True, stop=True)\
                    .then_inc(f_y1, 1)
                pe.wait_ge(f_g1, c + 1)
                pe.matmul(p_node2[0:D, 0:blocks * P], w2s[:, :], colw[0:D, 0, 0:blocks * P], start=True, stop=True)\
                    .then_inc(f_y2, 1)
                pe.wait_ge(f_s, c + 1)
                for b in range(blocks):
                    last = pe.transpose(p_node[:, b * D:(b + 1) * D], colv[0:D, 0, b * P:(b + 1) * P],
                                        ident[0:D, 0:D])
                last.then_inc(f_t, 1)
            groups(pe, gather_sum, lambda it: due(pe, it, final))
            rest(pe, final)

        @block.vector
        def _(v):
            v.sem_inc(e0.free, SLOTS - 1)
            v.sem_inc(e1.free, SLOTS - 1)
            v.sem_inc(a_peak, RING)
            v.memset(x1[:, N // P:NP // P, 0:D], 0.0).then_inc(s_fill, 1)
            v.memset(x1[:, :, D:D1], 1.0)
            v.memset(ones[:, :], 1.0)
            v.memset(run[:, :], 1.0)
            v.memset(zeros[:, :], 0.0)
            v.memset(no_node[:, :], -1)
            v.memset(fade[:, :, :], 1.0)
            v.memset(colw[D:D1, :, :], 1.0)
            v.memset(w0x[D:D1, D:D1], 1.0)
            v.memset(w0x[0:D, D:D1], 0.0).then_inc(s_fill, 1)

            v.wait_ge(s_fill, 2)
            v.wait_ge(s_w0, 16 * 3)
            v.tensor_scalar(att_wide[:, :], ones[0:D, :], att[:, 0:1], None, ALU.mult)
            v.wait_ge(s_prep, 1)
            v.tensor_copy(w0t[:, :], bank[7][0:D, 0:D]).then_inc(s_prepc, 1)
            v.wait_ge(s_prep, 2)
            v.tensor_copy(w0att[:, :], bank[7][0:D, 128:130]).then_inc(s_prepc, 1)
            v.wait_ge(s_prepc, 2)
            v.tensor_scalar(w0dst[:, :], ones[0:D, :], w0att[:, 1:2], None, ALU.mult)
            v.tensor_scalar(w0both[:, :], ones[0:D, :], w0att[:, 0:1], w0att[:, 1:2], ALU.mult, ALU.add)
            v.wait_ge(s_prep, 3)
            v.tensor_copy(w0src[:, :], bank[7][:, 256:256 + D]).then_inc(s_prepc, 1)
            v.wait_ge(s_prepc, 3)

            def rows_made(c, u, r):
                v.wait_ge(a_in, c + 1)
                chunk = x1[:, bass.ds(c * CB, CB), :]
                v.tensor_tensor(by_block(rowu[:, u, :]), chunk[:, :, 0:D],
                                w0src[:, None, :].broadcast_to([P, CB, D]), ALU.mult).then_inc(a_v, 1)
                v.wait_ge(a_v, c + 1)
                v.tensor_reduce(chunk[:, :, D1], by_block(rowu[:, u, :]), AX.X, ALU.add).then_inc(a_row, 1)

            def spans():
                v.wait_ge(s_dsts, 64)
                v.wait_ge(s_const, 3)
                v.tensor_reduce(low[:, :], dsts[:, :, :], AX.X, ALU.min)
                v.tensor_reduce(high[:, :], dsts[:, :, :], AX.X, ALU.max).then_inc(s_v, 1)
                v.wait_ge(s_v, 1)
                v.tensor_tensor(high[:, :], high[:, :], low[:, :], ALU.subtract).then_inc(s_v, 1)
                v.wait_ge(s_v, 2)
                v.tensor_tensor(more[:, :, :], high[:, :, None].broadcast_to([TG, 2, MAXW]),
                                steps_i[:, None, :].broadcast_to([TG, 2, MAXW]), ALU.is_ge).then_inc(s_v, 1)
                v.tensor_tensor(begun[:, :, :], low[:, None, :].broadcast_to([TG, MCHUNKS, 2]),
                                chunk_end[:, :, None].broadcast_to([TG, MCHUNKS, 2]), ALU.is_lt).then_inc(s_v, 1)
                v.wait_ge(s_v, 4)
                v.tensor_tensor(begun[:, :, :], begun[:, :, :], group_no[:, None, :].broadcast_to([TG, MCHUNKS, 2]),
                                ALU.mult)
                v.tensor_reduce(extra[:, :], more[:, :, :], AX.X, ALU.add).then_inc(s_tab0, 1)
            def stage(c, u, r):
                v.tensor_copy(by_block(xs[:, u, :]), x1[:, bass.ds(c * CB, CB), 0:D]).then_inc(a_x, 1)

            def peaks(c, u, r):
                v.wait_ge(a_colc, c + 1)
                v.tensor_tensor(peak[:, columns(c)], bank[3 + u][:, :], zcol[:, u, :], ALU.max).then_inc(a_peak, 1)
            chunks(v, (8, rows_made), (2, stage), (0, peaks), enter=spans)

            v.wait_ge(s_line, 1)
            v.tensor_reduce(begun_col[:, :], p_begun, AX.X, ALU.max)
            v.tensor_copy(line[:, :, :].rearrange("p a g -> p (a g)"), p_line).then_inc(s_begun, 1)
            v.wait_ge(s_begun, 1)
            v.tensor_copy(win_tab[:, 1, 0:GROUPS], line[:, 1, :])
            v.scalar_tensor_tensor(win_tab[:, 0, 0:GROUPS], line[:, 1, :], float(1 << BITS), line[:, 0, :], ALU.mult, ALU.add)
            v.tensor_tensor_scan(upto[:, :], run[:, :], line[:, 1, :], 0.0, ALU.mult, ALU.add).then_inc(s_v, 1)
            v.wait_ge(s_v, 5)
            v.tensor_tensor(win_tab[:, 2, 0:GROUPS], upto[:, :], line[:, 1, :], ALU.subtract).then_inc(s_tab, 1)
            v.wait_ge(s_since, 1)
            v.wait_ge(s_const, 5)
            v.tensor_reduce(since[:, :], p_since.rearrange("p (c k) -> p c k", k=2), AX.X, ALU.max).then_inc(s_v, 1)
            v.wait_ge(s_v, 6)
            v.tensor_tensor(ready[:, :, :], since[:, None, :].broadcast_to([1, ROUNDS, MCHUNKS]),
                            iota[0:1, SLOTS - 1:GROUPS - 1:SLOTS][:, :, None].broadcast_to([1, ROUNDS, MCHUNKS]),
                            ALU.is_le).then_inc(s_v, 1)
            v.memset(ready_n[:, 0:1], 0.0)
            v.memset(ready_n[:, ROUNDS + 1:ROUNDS + 2], float(MCHUNKS))
            v.wait_ge(s_v, 7)
            v.tensor_reduce(ready_n[:, 1:ROUNDS + 1], ready[:, :, :], AX.X, ALU.add).then_inc(s_v, 1)
            v.wait_ge(s_v, 8)
            v.scalar_tensor_tensor(due_tab[:, :], ready_n[:, 0:ROUNDS + 1], DUE - 1.0, ready_n[:, 1:ROUNDS + 2],
                                   ALU.mult, ALU.add).then_inc(s_tab, 1)
            v.wait_ge(s_tab, 2)

            v.wait_ge(a_peak, CHUNKS + RING)
            prev_reg = v.alloc_register("prev_window")
            now_reg = v.alloc_register("window")
            at_reg = v.alloc_register("at_window")

            def load_window(g):
                return v.value_load(win_tab[0:1, 0, bass.ds(g, 1)], min_val=0, max_val=(MAXW + 1) << BITS)

            windows = {}

            def set_window(before, now, u):
                if u == 0:
                    v.reg_mov(prev_reg, before)
                    v.reg_mov(now_reg, now)
                else:
                    windows["before"], windows["now"] = before, now

            def window(u, name):
                if u == 0:
                    windows["before"] = v.snap(prev_reg, min_val=0, max_val=N - 1)
                    windows["now"] = v.snap(now_reg, min_val=0, max_val=(MAXW + 1) << BITS)
                now = windows["now"]
                lo_reg, further_reg = v.alloc_register(f"lo_{name}"), v.alloc_register(f"further_{name}")
                v.reg_alu(lo_reg, now, (1 << BITS) - 1, ALU.bitwise_and)
                v.reg_alu(further_reg, now, BITS, ALU.logical_shift_right)
                lo = v.snap(lo_reg, True, min_val=0, max_val=N - 1)
                further = v.snap(further_reg, True, min_val=0, max_val=MAXW)
                return lo, further, windows["before"]

            def scores(st, lo, u):
                st.link(v.tensor_tensor(by_tile(other[:, :]), over_window(dst_i[:, u, :]),
                                        over_tiles(iota[:, bass.ds(lo, WIN)]), ALU.not_equal))
                st.link(v.scalar_tensor_tensor(by_tile(other[:, :]), by_tile(other[:, :]), NEG,
                                               over_window(rows0(u)[:, :, D1]), ALU.mult, ALU.add))

            def largest(t):
                v.tensor_reduce(top[:, :], other[:, :].rearrange("p (j n) -> p n j", j=TILES), AX.X, ALU.max)\
                    .then_inc(t.top, 1)

            def shift(st, lo):
                st.step(v.tensor_tensor(by_tile(score[:, :]), by_tile(other[:, :]),
                                        over_tiles(adst[:, bass.ds(lo, WIN)]), ALU.add))

            def new_peak(st, t, n, lo, p_top_, p_topb_, ahead=None):
                here = bass.ds(lo, WIN)
                v.wait_ge(t.topt, n)
                st.link(v.tensor_reduce(top_col[:, :], p_top_, AX.X, ALU.max))
                v.tensor_scalar(top_diag[:, :], ident[0:WIN, 0:WIN], top_col[:, 0:1], None, ALU.mult)\
                    .then_inc(t.diag, 1)
                v.scalar_tensor_tensor(score[:, :], score[:, :], SLOPE, score[:, :], ALU.mult, ALU.max)
                v.wait_ge(t.topb, n)
                st.link(v.tensor_tensor(cand[:, :], p_topb_, adst[:, here], ALU.add))
                st.link(v.scalar_tensor_tensor(cand[:, :], cand[:, :], SLOPE, cand[:, :], ALU.mult, ALU.max))
                st.link(v.tensor_tensor(newp[:, :], cand[:, :], peak[:, here], ALU.max))
                st.step(v.tensor_tensor(drop[:, :], peak[0:D1, here], newp[0:D1, :], ALU.subtract))
                v.tensor_tensor(by_tile(score[:, :]), by_tile(score[:, :]), over_tiles(newp[:, :]), ALU.subtract)\
                    .then_inc(t.score, 1)
                got = ahead() if ahead else None
                st.wait()
                st.step(v.tensor_tensor(peak[:, here], cand[:, :], peak[:, here], ALU.max))
                return got

            STEPS0 = 9
            STEPSX = 11

            def attend(g, it, u):
                lo, further, prev = window(u, f"0_{u}_{g is LAST}")
                st = Steps(v, e0.v, g * STEPS0, STEPS0)
                v.wait_ge(t0.away, g + 1)
                v.wait_ge(e0.rows[u], gathered(g, it))
                st.link(v.scalar_tensor_tensor(by_tile(other[:, :]), by_tile(onehot[:, u, :]), -1.0,
                                               over_window(rows0(u)[:, :, D1]), ALU.mult, ALU.add))
                largest(t0)
                v.wait_ge(t0.w, g + 1)
                shift(st, lo)
                after = new_peak(st, t0, g + 1, lo, p_top, p_topb, None if g is LAST else lambda: load_window(g + 1))
                before_here = bass.ds(prev, WIN)
                st.link(v.tensor_tensor(acc[:, before_here], acc[:, before_here], fade[:, (u - 1) % SLOTS, :], ALU.mult))
                v.wait_ge(e0.acc, g + 1)
                v.tensor_tensor(acc[:, before_here], acc[:, before_here], p_acc0, ALU.add).then_inc(e0.free, 1)
                st.done()
                with v.If(further > 0):
                    before = v.value_load(win_tab[0:1, 2, bass.ds(g, 1)], min_val=0, max_val=GROUPS * MAXW)
                    v.reg_mov(at_reg, lo)
                    with v.Fori(0, further) as k:
                        v.wait_ge(t0.w, g + 2)
                        v.reg_add(at_reg, at_reg, WIN)
                        at = v.snap(at_reg, min_val=0, max_val=N - 1)
                        n = v.snap(before + k, min_val=0, max_val=GROUPS * MAXW)
                        sx = Steps(v, x0_v, n * STEPSX, STEPSX)
                        scores(sx, at, u)
                        largest(tx)
                        shift(sx, at)
                        new_peak(sx, tx, n + 1, at, px_top, px_topb)
                        v.wait_ge(x0_acc, n + 1)
                        sx.link(v.tensor_tensor(acc[:, bass.ds(at, WIN)], acc[:, bass.ds(at, WIN)], fade_x[:, :], ALU.mult))
                        sx.link(v.tensor_tensor(acc[:, bass.ds(at, WIN)], acc[:, bass.ds(at, WIN)], px_acc0, ALU.add))
                        sx.done()
                if g is not LAST:
                    set_window(lo, after, (u + 1) % SLOTS)
                return lo

            def normed(st, y, blocks, made, rooted, n, to, given):
                for b in range(blocks):
                    last = v.bn_stats(bst[:, b, :], y[:, b, :])
                st.link(last)
                v.sem_inc(s_mark, 1)
                for b in range(blocks):
                    last = v.bn_aggr(mv[:, 0, 2 * b:2 * b + 2], bst[:, b, :])
                st.link(last)
                here = slice(0, blocks)
                v.tensor_scalar(var[:, 0, here], mv[:, 0, :].rearrange("p (b k) -> p b k", k=2)[:, here, 1], EPS, None,
                                ALU.add).then_inc(made, 1)
                v.wait_ge(rooted, n)
                st.link(v.reciprocal(rstd[:, 0, here], var[:, 1, here]))
                st.link(v.scalar_tensor_tensor(newton[:, here], var[:, 0, here], -0.5, rstd[:, 0, here],
                                               ALU.mult, ALU.mult))
                st.link(v.tensor_tensor(newton[:, here], newton[:, here], rstd[:, 0, here], ALU.mult))
                st.link(v.scalar_tensor_tensor(rstd[:, 0, here], newton[:, here], 1.5, rstd[:, 0, here],
                                               ALU.add, ALU.mult))
                for b in range(blocks):
                    last = v.tensor_scalar(to[:, b, :], y[:, b, :], mv[:, 0, 2 * b:2 * b + 1], rstd[:, 0, b:b + 1],
                                           ALU.subtract, ALU.mult)
                last.then_inc(given, 1)

            def middle(c, blocks=MB):
                st = Steps(v, m_v, c * 8, 8)
                v.tensor_copy(colv[:, 0, 0:blocks * P], acc[:, nodes(c, blocks)]).then_inc(m_col, 1)
                v.wait_ge(m_t, c + 1)
                st.link(v.tensor_scalar(den[:, 0, 0:blocks], by_block(p_node[:, :], D1)[:, 0:blocks, D], 1e-16, None,
                                        ALU.add))
                v.reciprocal(rden[:, 0, 0:blocks], den[:, 0, 0:blocks]).then_inc(m_rden, 1)
                v.wait_ge(m_th, c + 1)
                y = by_block(rowu[:, 0, :])[:, 0:blocks, :]
                st.link(v.tensor_tensor(y, y, x1[:, bass.ds(c * MB, blocks), 0:D], ALU.add))
                normed(st, y, blocks, m_var, m_dev, c + 1, by_block(xs[:, 0, :]), m_x1)
                st.done()

            def middle_due(it):
                v.wait_ge(e0.free, it * SLOTS + 2 * SLOTS - 1)
                due(v, it, middle)

            set_window(0, load_window(0), 0)
            prev = groups(v, attend, middle_due)
            v.wait_ge(e0.acc, GROUPS + 1)
            v.tensor_tensor(acc[:, bass.ds(prev, WIN)], acc[:, bass.ds(prev, WIN)], fade[:, 0, :], ALU.mult).then_inc(s_v, 1)
            v.wait_ge(s_v, 9)
            v.tensor_tensor(acc[:, bass.ds(prev, WIN)], acc[:, bass.ds(prev, WIN)], p_acc0, ALU.add).then_inc(e0.free, 1)

            v.wait_ge(e0.free, GROUPS + SLOTS)
            rest(v, middle)
            v.wait_ge(m_colw, MCHUNKS + 1)

            def message(g, it, u):
                lo, further, prev = window(u, f"1_{u}_{g is LAST}")
                v.wait_ge(e1.dst[u], 16 * (it + 1))
                v.tensor_tensor(by_tile(onehot[:, u, :]), over_window(dst_i[:, u, :]),
                                over_tiles(iota[:, bass.ds(lo, WIN)]), ALU.is_equal).then_inc(e1_hot, 1)
                v.wait_ge(e1.rows[u], gathered(g, it))
                v.wait_ge(e1.attr[u], 16 * (it + 1))
                v.tensor_tensor(rows[:, u, 0:TILES * D], rows[:, u, 0:TILES * D], attr[:, u, :], ALU.mult)\
                    .then_inc(e1_msg, 1)
                v.wait_ge(e1.free, g + SLOTS - 1)
                v.wait_ge(e1.acc, g + 1)
                here = bass.ds(prev, WIN)
                v.tensor_tensor(acc[0:D, here], acc[0:D, here], p_acc1[(u - 1) % SLOTS], ALU.add).then_inc(e1.free, 1)
                after = None if g is LAST else load_window(g + 1)
                with v.If(further > 0):
                    before = v.value_load(win_tab[0:1, 2, bass.ds(g, 1)], min_val=0, max_val=GROUPS * MAXW)
                    v.reg_mov(at_reg, lo)
                    with v.Fori(0, further) as k:
                        v.reg_add(at_reg, at_reg, WIN)
                        at = v.snap(at_reg, min_val=0, max_val=N - 1)
                        v.tensor_tensor(by_tile(onehot_x[:, :]), over_window(dst_i[:, u, :]),
                                        over_tiles(iota[:, bass.ds(at, WIN)]), ALU.is_equal).then_inc(x1_hot, 1)
                        v.wait_ge(x1_acc, before + k + 1)
                        v.wait_ge(e1.free, g + SLOTS)
                        v.tensor_tensor(acc[0:D, bass.ds(at, WIN)], acc[0:D, bass.ds(at, WIN)], px_acc1, ALU.add)\
                            .then_inc(x1_v, 1)
                        v.wait_ge(x1_v, before + k + 1)
                if g is not LAST:
                    set_window(lo, after, (u + 1) % SLOTS)
                return lo

            def final(c, blocks=MB):
                st = Steps(v, f_v, c * 7, 7)
                v.sem_inc(f_go, 1)
                v.wait_ge(f_g2, c + 1)
                v.tensor_tensor(colv[0:D, 0, 0:blocks * P], colv[0:D, 0, 0:blocks * P], acc[0:D, nodes(c, blocks)],
                                ALU.add).then_inc(f_s, 1)
                v.wait_ge(f_t, c + 1)
                y = by_block(rowu[:, 0, :])[:, 0:blocks, :]
                st.link(v.tensor_tensor(y, by_block(p_node[:, :])[:, 0:blocks, :], x1[:, bass.ds(c * MB, blocks), 0:D],
                                        ALU.add))
                normed(st, y, blocks, f_var, f_dev, c + 1, by_block(rowt[:, 0, :]), f_o)
                v.wait_ge(f_o, c + 1)
                st.done()

            def final_due(it):
                v.wait_ge(e1.free, it * SLOTS + 2 * SLOTS - 1)
                due(v, it, final)

            set_window(0, load_window(0), 0)
            prev = groups(v, message, final_due)
            v.wait_ge(e1.acc, GROUPS + 1)
            v.wait_ge(e1.free, GROUPS + SLOTS - 1)
            v.tensor_tensor(acc[0:D, bass.ds(prev, WIN)], acc[0:D, bass.ds(prev, WIN)], p_acc1[0], ALU.add)\
                .then_inc(e1.free, 1)
            v.wait_ge(e1.free, GROUPS + SLOTS)

            rest(v, final)


_INS = ['x', 'src', 'dst', 'edge_attr_96', 'L0_gnn_W', 'L0_gnn_att_src', 'L0_gnn_att_dst', 'L0_gnn_bias',
        'L1_gnn_W_pre', 'L1_gnn_b_pre', 'L1_gnn_W1', 'L1_gnn_b1', 'L1_gnn_W2', 'L1_gnn_b2']


def kernel(**inputs):
    import numpy as _np
    import concourse.bacc as _bacc
    from concourse import mybir as _mybir
    from concourse.bass_utils import run_bass_kernel_spmd as _run

    nc = _bacc.Bacc("TRN2", target_bir_lowering=False, num_devices=1)
    arrays, args = {}, []
    for name in _INS:
        a = _np.ascontiguousarray(inputs[name])
        arrays[f"in_{name}_dram"] = a
        args.append(nc.dram_tensor(f"in_{name}_dram", a.shape, _mybir.dt.from_np(a.dtype), kind="ExternalInput").ap())
    shape = inputs['x'].shape
    args.append(nc.dram_tensor("out_0_dram", shape, _mybir.dt.float32, kind="ExternalOutput").ap())
    gnn(nc, *args)
    r = _run(nc, [arrays], core_ids=[0])
    return r.results[0]["out_0_dram"]
```
